# Optimizing a Trainium2 kernel written in Bass

```python
import numpy as np
import jax
import jax.numpy as jnp

def _softmax(x, axis=-1):
    return jax.nn.softmax(x, axis=axis)
def _gelu(x):
    return jax.nn.gelu(x, approximate=True)
def _silu(x):
    return jax.nn.silu(x)
def _sigmoid(x):
    return jax.nn.sigmoid(x)
def _layernorm(x, axis=-1, eps=1e-5):
    m = jnp.mean(x, axis=axis, keepdims=True)
    v = jnp.var(x, axis=axis, keepdims=True)
    return (x - m) / jnp.sqrt(v + eps)
def _scatter_add(tgt, idx, src, axis=0):
    return tgt.at[idx].add(src)
def _segment_sum(src, seg, n):
    return jax.ops.segment_sum(src, seg, n)

kernel_name = 'mk_conv_seq_d2_conv_nchw128_335c05'

def setup_inputs(seed: int = 0):
    np.random.seed(seed)
    _w = jnp.asarray
    def _rec_inputs():
        import jax
        import jax.numpy as jnp
        _gk = jax.random.key(seed)
        x = -0.0002023 + 1 * jax.random.normal(jax.random.fold_in(_gk, 1), (16, 128, 56, 56), jnp.float32)
        return x
    x = _rec_inputs()
    def _L0_conv_setup():
        import jax, jax.numpy as jnp
        import numpy as np
        B, C, H, W = (16, 128, 56, 56)
        QK, HEADS, NWIN, TOPK, MLPR = (128, 4, 7, 4, 3)
        HD_Q, HD_V = (QK // HEADS, C // HEADS)
        WH, WW = (H // NWIN, W // NWIN)
        P2, W2 = (NWIN * NWIN, WH * WW)
        SCALE = QK ** (-0.5)

        def _dwconv(x, w, b):
            y = jax.lax.conv_general_dilated(x, w, (1, 1), 'SAME', feature_group_count=x.shape[1], dimension_numbers=('NCHW', 'OIHW', 'NCHW'))
            return y + b[None, :, None, None]

        def _ln(x, g, b):
            m = x.mean(-1, keepdims=True)
            v = ((x - m) ** 2).mean(-1, keepdims=True)
            return (x - m) * jax.lax.rsqrt(v + 1e-06) * g + b

        def _win(t):
            b, _, _, c = t.shape
            return t.reshape(b, NWIN, WH, NWIN, WW, c).transpose(0, 1, 3, 2, 4, 5).reshape(b, P2, WH, WW, c)

        def _unwin(t):
            b, c = (t.shape[0], t.shape[-1])
            return t.reshape(b, NWIN, NWIN, WH, WW, c).transpose(0, 1, 3, 2, 4, 5).reshape(b, H, W, c)
        key = jax.random.key(seed)
        ks = jax.random.split(key, 8)
        p = lambda k, sh: (0.02 * jax.random.normal(k, sh)).astype(jnp.float32)
        return {'x': jax.random.normal(ks[0], (B, C, H, W), dtype=jnp.float32), 'pos_w': p(ks[1], (C, 1, 3, 3)), 'pos_b': jnp.zeros((C,), jnp.float32), 'ln1_g': jnp.ones((C,), jnp.float32), 'ln1_b': jnp.zeros((C,), jnp.float32), 'qkv_w': p(ks[2], (C, 2 * QK + C)), 'qkv_b': jnp.zeros((2 * QK + C,), jnp.float32), 'lepe_w': p(ks[3], (C, 1, 5, 5)), 'lepe_b': jnp.zeros((C,), jnp.float32), 'wo_w': p(ks[4], (C, C)), 'wo_b': jnp.zeros((C,), jnp.float32), 'ln2_g': jnp.ones((C,), jnp.float32), 'ln2_b': jnp.zeros((C,), jnp.float32), 'mlp_w1': p(ks[5], (C, MLPR * C)), 'mlp_b1': jnp.zeros((MLPR * C,), jnp.float32), 'mlp_w2': p(ks[6], (MLPR * C, C)), 'mlp_b2': jnp.zeros((C,), jnp.float32)}
    _L0_conv_all = _L0_conv_setup()
    _L0_conv_in = {k: v for k, v in _L0_conv_all.items() if k in ('pos_w', 'pos_b', 'ln1_g', 'ln1_b', 'qkv_w', 'qkv_b', 'lepe_w', 'lepe_b', 'wo_w', 'wo_b', 'ln2_g', 'ln2_b', 'mlp_w1', 'mlp_b1', 'mlp_w2', 'mlp_b2', )}
    del _L0_conv_all

    def _L1_conv_setup():
        import jax, jax.numpy as jnp
        import numpy as np
        from jax import lax
        EPS = 1e-05

        def _conv3x3(x, w):
            return lax.conv_general_dilated(x, w, window_strides=(1, 1), padding=((1, 1), (1, 1)), dimension_numbers=('NCHW', 'OIHW', 'NCHW'))

        def _batchnorm(y, gamma, beta):
            mean = jnp.mean(y, axis=(0, 2, 3), keepdims=True)
            var = jnp.var(y, axis=(0, 2, 3), keepdims=True)
            inv = lax.rsqrt(var + EPS)
            return (y - mean) * inv * gamma[None, :, None, None] + beta[None, :, None, None]
        key = jax.random.key(seed)
        k1, k2, k3 = jax.random.split(key, 3)
        N, C, H, W = (32, 128, 56, 56)
        x = jax.random.normal(k1, (N, C, H, W), dtype=jnp.float32)
        w1 = jax.random.normal(k2, (C, C, 3, 3), dtype=jnp.float32) * 0.05
        w2 = jax.random.normal(k3, (C, C, 3, 3), dtype=jnp.float32) * 0.05
        gamma1 = jnp.ones((C,), jnp.float32)
        beta1 = jnp.zeros((C,), jnp.float32)
        gamma2 = jnp.ones((C,), jnp.float32)
        beta2 = jnp.zeros((C,), jnp.float32)
        return {'x': x, 'w1': w1, 'gamma1': gamma1, 'beta1': beta1, 'w2': w2, 'gamma2': gamma2, 'beta2': beta2}
    _L1_conv_all = _L1_conv_setup()
    _L1_conv_in = {k: v for k, v in _L1_conv_all.items() if k in ('w1', 'gamma1', 'beta1', 'w2', 'gamma2', 'beta2', )}
    del _L1_conv_all

    return {
        "x": x,
        "L0_conv_pos_w": _L0_conv_in["pos_w"],
        "L0_conv_pos_b": _L0_conv_in["pos_b"],
        "L0_conv_ln1_g": _L0_conv_in["ln1_g"],
        "L0_conv_ln1_b": _L0_conv_in["ln1_b"],
        "L0_conv_qkv_w": _L0_conv_in["qkv_w"],
        "L0_conv_qkv_b": _L0_conv_in["qkv_b"],
        "L0_conv_lepe_w": _L0_conv_in["lepe_w"],
        "L0_conv_lepe_b": _L0_conv_in["lepe_b"],
        "L0_conv_wo_w": _L0_conv_in["wo_w"],
        "L0_conv_wo_b": _L0_conv_in["wo_b"],
        "L0_conv_ln2_g": _L0_conv_in["ln2_g"],
        "L0_conv_ln2_b": _L0_conv_in["ln2_b"],
        "L0_conv_mlp_w1": _L0_conv_in["mlp_w1"],
        "L0_conv_mlp_b1": _L0_conv_in["mlp_b1"],
        "L0_conv_mlp_w2": _L0_conv_in["mlp_w2"],
        "L0_conv_mlp_b2": _L0_conv_in["mlp_b2"],
        "L1_conv_w1": _L1_conv_in["w1"],
        "L1_conv_gamma1": _L1_conv_in["gamma1"],
        "L1_conv_beta1": _L1_conv_in["beta1"],
        "L1_conv_w2": _L1_conv_in["w2"],
        "L1_conv_gamma2": _L1_conv_in["gamma2"],
        "L1_conv_beta2": _L1_conv_in["beta2"],
    }

def reference(x, L0_conv_pos_w, L0_conv_pos_b, L0_conv_ln1_g, L0_conv_ln1_b, L0_conv_qkv_w, L0_conv_qkv_b, L0_conv_lepe_w, L0_conv_lepe_b, L0_conv_wo_w, L0_conv_wo_b, L0_conv_ln2_g, L0_conv_ln2_b, L0_conv_mlp_w1, L0_conv_mlp_b1, L0_conv_mlp_w2, L0_conv_mlp_b2, L1_conv_w1, L1_conv_gamma1, L1_conv_beta1, L1_conv_w2, L1_conv_gamma2, L1_conv_beta2):
    import jax
    import jax.numpy as jnp
    def _L0_conv_ref(x, pos_w, pos_b, ln1_g, ln1_b, qkv_w, qkv_b, lepe_w, lepe_b, wo_w, wo_b, ln2_g, ln2_b, mlp_w1, mlp_b1, mlp_w2, mlp_b2):
        import jax, jax.numpy as jnp
        import numpy as np
        B, C, H, W = (16, 128, 56, 56)
        QK, HEADS, NWIN, TOPK, MLPR = (128, 4, 7, 4, 3)
        HD_Q, HD_V = (QK // HEADS, C // HEADS)
        WH, WW = (H // NWIN, W // NWIN)
        P2, W2 = (NWIN * NWIN, WH * WW)
        SCALE = QK ** (-0.5)

        def _dwconv(x, w, b):
            y = jax.lax.conv_general_dilated(x, w, (1, 1), 'SAME', feature_group_count=x.shape[1], dimension_numbers=('NCHW', 'OIHW', 'NCHW'))
            return y + b[None, :, None, None]

        def _ln(x, g, b):
            m = x.mean(-1, keepdims=True)
            v = ((x - m) ** 2).mean(-1, keepdims=True)
            return (x - m) * jax.lax.rsqrt(v + 1e-06) * g + b

        def _win(t):
            b, _, _, c = t.shape
            return t.reshape(b, NWIN, WH, NWIN, WW, c).transpose(0, 1, 3, 2, 4, 5).reshape(b, P2, WH, WW, c)

        def _unwin(t):
            b, c = (t.shape[0], t.shape[-1])
            return t.reshape(b, NWIN, NWIN, WH, WW, c).transpose(0, 1, 3, 2, 4, 5).reshape(b, H, W, c)
        x = x + _dwconv(x, pos_w, pos_b)
        xh = x.transpose(0, 2, 3, 1)
        y = _ln(xh, ln1_g, ln1_b)
        qkv = y @ qkv_w + qkv_b
        q, kv = (qkv[..., :QK], qkv[..., QK:])
        qw, kvw = (_win(q), _win(kv))
        q_win = jax.lax.stop_gradient(qw.mean((2, 3)))
        k_win = jax.lax.stop_gradient(kvw[..., :QK].mean((2, 3)))
        logits = jnp.einsum('bpc,bqc->bpq', q_win * SCALE, k_win)
        _, idx = jax.lax.top_k(logits, TOPK)
        kv_pix = kvw.reshape(B, P2, W2, QK + C)
        kv_sel = jax.vmap(lambda t, i: t[i])(kv_pix, idx)
        k_sel = kv_sel[..., :QK].reshape(B, P2, TOPK * W2, HEADS, HD_Q)
        v_sel = kv_sel[..., QK:].reshape(B, P2, TOPK * W2, HEADS, HD_V)
        q_pix = qw.reshape(B, P2, W2, HEADS, HD_Q)
        att = jnp.einsum('bpqhd,bpkhd->bphqk', q_pix * SCALE, k_sel)
        att = jax.nn.softmax(att, axis=-1)
        o = jnp.einsum('bphqk,bpkhd->bpqhd', att, v_sel).reshape(B, P2, W2, C)
        o = _unwin(o)
        v_img = kv[..., QK:].transpose(0, 3, 1, 2)
        lepe = _dwconv(v_img, lepe_w, lepe_b).transpose(0, 2, 3, 1)
        o = (o + lepe) @ wo_w + wo_b
        xh = xh + o
        z = _ln(xh, ln2_g, ln2_b)
        z = jax.nn.gelu(z @ mlp_w1 + mlp_b1, approximate=False) @ mlp_w2 + mlp_b2
        xh = xh + z
        return xh.transpose(0, 3, 1, 2)

    def _L1_conv_ref(x, w1, gamma1, beta1, w2, gamma2, beta2):
        import jax, jax.numpy as jnp
        import numpy as np
        from jax import lax
        EPS = 1e-05

        def _conv3x3(x, w):
            return lax.conv_general_dilated(x, w, window_strides=(1, 1), padding=((1, 1), (1, 1)), dimension_numbers=('NCHW', 'OIHW', 'NCHW'))

        def _batchnorm(y, gamma, beta):
            mean = jnp.mean(y, axis=(0, 2, 3), keepdims=True)
            var = jnp.var(y, axis=(0, 2, 3), keepdims=True)
            inv = lax.rsqrt(var + EPS)
            return (y - mean) * inv * gamma[None, :, None, None] + beta[None, :, None, None]
        w1b = w1 + lax.stop_gradient(jnp.sign(w1) - w1)
        w2b = w2 + lax.stop_gradient(jnp.sign(w2) - w2)
        out = jax.nn.relu(_batchnorm(_conv3x3(x, w1b), gamma1, beta1))
        out = _batchnorm(_conv3x3(out, w2b), gamma2, beta2)
        out = out + x
        return jax.nn.relu(out)

    def _gn(v, G=32, eps=1e-5):
        B_, C_, H_, W_ = v.shape
        g = v.reshape(B_, G, C_ // G, H_, W_)
        m = jnp.mean(g, axis=(2, 3, 4), keepdims=True)
        s = jnp.var(g, axis=(2, 3, 4), keepdims=True)
        return ((g - m) / jnp.sqrt(s + eps)).reshape(v.shape)

    def _ln_c(v, eps=1e-6):
        m = jnp.mean(v, axis=1, keepdims=True)
        s = jnp.var(v, axis=1, keepdims=True)
        return (v - m) / jnp.sqrt(s + eps)

    def _ln_t(v, eps=1e-5):
        m = jnp.mean(v, axis=-1, keepdims=True)
        s = jnp.var(v, axis=-1, keepdims=True)
        return (v - m) / jnp.sqrt(s + eps)

    def _to_tokens(v):
        B_, C_, H_, W_ = v.shape
        return v.reshape(B_, C_, H_ * W_).transpose(0, 2, 1)
    def _from_tokens(t, like):
        B_, C_, H_, W_ = like.shape
        return t.transpose(0, 2, 1).reshape(B_, C_, H_, W_)

    x = _L0_conv_ref(x, L0_conv_pos_w, L0_conv_pos_b, L0_conv_ln1_g, L0_conv_ln1_b, L0_conv_qkv_w, L0_conv_qkv_b, L0_conv_lepe_w, L0_conv_lepe_b, L0_conv_wo_w, L0_conv_wo_b, L0_conv_ln2_g, L0_conv_ln2_b, L0_conv_mlp_w1, L0_conv_mlp_b1, L0_conv_mlp_w2, L0_conv_mlp_b2)
    x = _L1_conv_ref(x, L1_conv_w1, L1_conv_gamma1, L1_conv_beta1, L1_conv_w2, L1_conv_gamma2, L1_conv_beta2)
    return x


_drawn_inputs = setup_inputs


def setup_inputs(seed=0):
    import zlib

    import numpy as np

    out = dict(_drawn_inputs(seed))
    spreads = {'L0_conv_pos_b': (0.0, 0.1),
     'L0_conv_ln1_g': (1.0, 0.6),
     'L0_conv_ln1_b': (0.0, 0.8),
     'L0_conv_qkv_b': (0.0, 0.443),
     'L0_conv_lepe_b': (0.0, 0.455),
     'L0_conv_wo_b': (0.0, 0.1),
     'L0_conv_ln2_g': (1.0, 0.6),
     'L0_conv_ln2_b': (0.0, 2.0),
     'L0_conv_mlp_b1': (0.0, 0.526),
     'L0_conv_mlp_b2': (0.0, 0.1),
     'L1_conv_gamma1': (1.0, 0.2),
     'L1_conv_beta1': (0.0, 0.1),
     'L1_conv_gamma2': (1.0, 0.2),
     'L1_conv_beta2': (0.0, 0.1)}
    factors = {'L0_conv_qkv_w': 7.085, 'L0_conv_lepe_w': 8.0}
    for name, (base, spread) in spreads.items():
        noise = np.random.default_rng([zlib.crc32(name.encode()), seed]).standard_normal(out[name].shape)
        drawn = base * np.exp(spread * noise) if base else spread * noise
        out[name] = jnp.asarray(drawn.astype(out[name].dtype))
    for name, factor in factors.items():
        out[name] = (out[name] * factor).astype(out[name].dtype)
    return out
```

```python
from contextlib import ExitStack

import numpy as np

import concourse.bass as bass
from concourse import mybir

F32 = mybir.dt.float32
F32R = mybir.dt.float32r
U32 = mybir.dt.uint32
ALU = mybir.AluOpType
ACT = mybir.ActivationFunctionType
AX = mybir.AxisListType

P = 128
H = W = 56
PIX = H * W
NWIN = 7
WIN = 8
WPIX = WIN * WIN
NW = NWIN * NWIN
STRIP = WIN * W
HEADS, HD = 4, 32
TOPK = 4
KEYS = TOPK * WPIX
PAIR = 2 * WPIX
HID = 3
SCALE = float(P) ** -0.5
LN_EPS = 1e-6
BN_EPS = 1e-5
LT = 112
NLT = PIX // LT
LPS = STRIP // LT

SHIFTS = [(0, 0), (0, 2), (0, 3), (1, 0)]
PLACES = [(0, 0), (0, 1), (1, 0), (1, 2), (2, 1), (3, 0), (3, 2), (4, 1)]
NS, NP = len(SHIFTS), len(PLACES)
VW = W + 4
VROWS = H + 6
RLEN = (WIN + 4) * VW
CW = W + 2
TAPS3 = [(dy, dx) for dy in (-1, 0, 1) for dx in (-1, 0, 1)]

VEC = {}
_n = 0
for _name, _k in [("pos_w", 9), ("pos_b", 1), ("ln1_g", 1), ("ln1_b", 1), ("qkv_b", 3), ("lepe_b", 1),
                  ("wo_b", 1), ("ln2_g", 1), ("ln2_b", 1), ("mlp_b1", HID), ("mlp_b2", 1), ("gamma1", 1),
                  ("beta1", 1), ("gamma2", 1), ("beta2", 1), ("lepe_taps", HEADS * NP)]:
    VEC[_name] = _n
    _n += _k
NVEC = _n


def lepe_cover():
    taken, out = set(), []
    for ty, tx in PLACES:
        row = []
        for sy, sx in SHIFTS:
            tap = (ty + sy, tx + sx)
            new = tap[0] < 5 and tap[1] < 5 and tap not in taken
            if new:
                taken.add(tap)
            row.append(tap if new else None)
        out.append(row)
    assert len(taken) == 25
    return out


def build(nc, x, vec, wqkv, wo, w1, w2, cw1, cw2, eye, centre, eye4, out, nb, dump=None):
    x3_dram = nc.dram_tensor("x3_scratch", [nb, P, PIX], F32).ap()
    y1_dram = nc.dram_tensor("y1_scratch", [nb, P, PIX], F32).ap()
    y2_dram = nc.dram_tensor("y2_scratch", [nb, P, PIX], F32).ap()

    with ExitStack() as ctx:
        def sb(name, shape, dt=F32):
            return ctx.enter_context(nc.sbuf_tensor(name, shape, dt))

        def sem(name):
            return ctx.enter_context(nc.semaphore(name))

        ps = ctx.enter_context(nc.psum_tensor("ps", [P, 8, 512], F32))

        vec_sb = sb("vec_sb", [P, NVEC])
        eye_sb = sb("eye_sb", [P, P])
        centre_sb = sb("centre_sb", [P, P])
        eye4_sb = sb("eye4_sb", [P, HD])
        mean_col = sb("mean_col", [P, 1])
        eps_col = sb("eps_col", [P, 2])
        wqkv_sb = sb("wqkv_sb", [P, 3 * P])
        wo_sb = sb("wo_sb", [P, P])
        w1_sb = sb("w1_sb", [P, HID * P])
        w2_sb = sb("w2_sb", [P, HID, P])
        cw_sign = sb("cw_sign", [P, 9, P], F32R)
        lepe_sb = sb("lepe_sb", [P, HEADS * NP, HD])
        bias = sb("bias", [P, 10])
        bq, bk, bv = (bias[:, i:i + 1] for i in range(3))
        bh = [bias[:, 3 + c:4 + c] for c in range(HID)]
        b_lepe = bias[:, 6:7]
        pos_centre = bias[:, 7:8]

        def v_(name, i=0):
            return vec_sb[:, VEC[name] + i:VEC[name] + i + 1]

        arena = sb("arena", [P, 6 * PIX])
        xin = arena[:, 0:PIX]
        x1 = arena[:, PIX:2 * PIX]
        x2 = arena[:, 2 * PIX:3 * PIX]
        xc = arena[:, 3 * PIX:4 * PIX]
        xhat = arena[:, 4 * PIX:5 * PIX]
        k_sb = arena[:, 5 * PIX:6 * PIX]
        q_sb = sb("q_sb", [P, 2, NWIN, HEADS, WPIX])
        vpad = sb("vpad", [P, VROWS * VW])
        shifted = sb("shifted", [P, 2, HEADS, RLEN])
        hid = shifted[:, :, 0:2, :].rearrange("p a g n -> p a (g n)")[:, :, 0:HID * STRIP].rearrange(
            "p a (c n) -> p a c n", c=HID)
        sq = hid[:, :, 0, :]
        vt = sb("vt", [P, NW * P])
        vsel = sb("vsel", [P, 2, 2, P])
        probs = sb("probs", [P, 2, 2, KEYS])
        probs_t = sb("probs_t", [P, 4 * P])
        neg_max = sb("neg_max", [P, 2, 2])
        row_sum = sb("row_sum", [P, 2, 2])
        row_inv = sb("row_inv", [P, 2, 2])
        lp = probs[:, :, :, :].rearrange("p a b k -> p a (b k)")[:, :, 0:STRIP]
        ln_small = sb("ln_small", [LT, 2, NLT])
        rstd_t = sb("rstd_t", [NLT, LT])
        win_sum = sb("win_sum", [P, NW])
        qk_win = sb("qk_win", [P, 2, NW])
        logits = sb("logits", [NW, NW])
        top8 = sb("top8", [NW, 8])
        top_i = sb("top_i", [NW, 8], U32)
        top_off = sb("top_off", [NW, TOPK], U32)
        key_off = sb("key_off", [1, NW * TOPK], U32)
        hi = sb("hi", [P, CW * CW], F32R)
        lo = sb("lo", [P, CW * CW], F32R)
        stats = sb("stats", [P, nb * NWIN, 6])
        bn_sb = sb("bn_sb", [P, 6])

        def img(t, s):
            return t[:, s * STRIP:(s + 1) * STRIP].rearrange("p (r x c) -> p r x c", r=WIN, c=WIN)

        def win(t, s):
            return t[:, s * STRIP:(s + 1) * STRIP].rearrange("p (x r c) -> p r x c", r=WIN, c=WIN)

        def inner(t, s):
            return t[:, :].rearrange("p (h w) -> p h w", w=CW)[:, 1 + WIN * s:1 + WIN * (s + 1), 1:1 + W]

        def rows(t, s):
            return t[:, s * STRIP:(s + 1) * STRIP].rearrange("p (r w) -> p r w", w=W)

        S = {n: sem(n) for n in (
            "setup_loaded", "setup_dve", "setup_pe", "x_loaded", "pos_done",
            "centred", "centred_copied", "squares", "variances", "eps_added", "roots", "rstd", "rstd_turned",
            "rstd_rows", "rstd_spread", "normed",
            "k_made", "v_made", "vt_made", "k_kept", "v_kept", "vt_kept",
            "win_sums", "win_qk_made", "win_qk_kept", "logits_made", "logits_kept", "top_values", "top_found",
            "offsets", "offsets_placed",
            "q_made", "q_kept", "scores_made", "max_found", "exp_done", "inv_done", "probs_scaled",
            "probs_turned", "turned_kept", "v_chosen", "mixed", "mixed_kept",
            "shifted0", "shifted1", "lepe_made", "lepe_kept", "projected", "x2_done",
            "hidden_made", "hidden_kept", "mlp_made", "x3_done", "hi_done", "lo_done",
            "conv_made", "conv_kept", "conv_stats", "x3_stored", "y1_stored",
            "b_loaded0", "b_loaded1", "relu_done", "b_hi", "b_lo", "b_made", "b_kept", "b_stats", "b_stored0",
            "b_stored1", "bn_dve", "bn_act", "c_loaded0", "c_loaded1", "c_sum", "c_relu", "c_stored0",
            "c_stored1", "pad_zero", "signs2_loaded", "held")}

        ns = len(SHIFTS) * HEADS * 16
        SLOT_STRIPS = (4, 3)

        block = ctx.enter_context(nc.Block())

        def hold(e, which, value):
            e.wait_ge(which, value)
            e.sem_inc(S["held"], 1)

        def image_loop(e, body):
            if nb > 1:
                with e.Fori(0, nb - 1) as b:
                    body(b, False)
            body(nb - 1, True)

        def window_rows(e, step):
            with e.Fori(0, NWIN // 2) as t:
                for half in range(2):
                    for j in range(NWIN):
                        step(2 * t + half, half, j, False)
            for j in range(NWIN):
                step(NWIN - 1, 0, j, True)

        @block.sync
        def _(e):
            loads = [(vec_sb, vec), (eye_sb, eye), (centre_sb, centre), (eye4_sb, eye4), (wqkv_sb, wqkv),
                     (wo_sb, wo), (w1_sb, w1)]
            for dst, src in loads:
                e.dma_start(dst[:, :], src).then_inc(S["setup_loaded"], 16)
            e.dma_start(w2_sb[:, :, :], w2.rearrange("(c p) n -> p c n", p=P)).then_inc(S["setup_loaded"], 16)
            e.dma_start(xhat[:, 0:9 * P], cw1).then_inc(S["setup_loaded"], 16)
            e.dma_start(xin, x[0]).then_inc(S["x_loaded"], 16)

            def image(b, last):
                if not last:
                    e.wait_ge(S["pos_done"], b * 9 + 9)
                    e.dma_start(xin, x[bass.ds(b + 1, 1)].rearrange("a p n -> (a p) n")).then_inc(S["x_loaded"], 16)
                e.wait_ge(S["offsets"], b + 1)
                e.dma_start(key_off[0:1, :], top_off[:, :]).then_inc(S["offsets_placed"], 16)
                e.wait_ge(S["v_kept"], b * NWIN + NWIN)
                for s in range(NWIN):
                    if s >= 2:
                        e.wait_ge(S["lepe_made"], b * NWIN + s - 1)
                    for k, (sy, sx) in enumerate(SHIFTS):
                        for g in range(HEADS):
                            at = WIN * s * VW + sy * VW + sx
                            e.dma_start(shifted[HD * k:HD * k + HD, s % 2, g, :],
                                        vpad[HD * g:HD * g + HD, at:at + RLEN]).then_inc(S[f"shifted{s % 2}"], 16)
                e.wait_ge(S["x3_done"], b * NWIN + NWIN)
                e.dma_start(x3_dram[bass.ds(b, 1)].rearrange("a p n -> (a p) n"), x2).then_inc(S["x3_stored"], 16)
                e.wait_ge(S["conv_kept"], b * NWIN + NWIN)
                e.dma_start(y1_dram[bass.ds(b, 1)].rearrange("a p n -> (a p) n"), xc).then_inc(S["y1_stored"], 16)

            for name in ("x3_stored", "y1_stored", "b_stored0", "b_stored1"):
                e.sem_inc(S[name], 16)
            image_loop(e, image)

            def part_b(b, i):
                yin, yout = arena[:, i * PIX:(i + 1) * PIX], arena[:, (2 + i) * PIX:(3 + i) * PIX]
                return yin, yout
            e.wait_ge(S["hidden_made"], 3 * NWIN * nb)
            e.dma_start(xhat[:, 0:9 * P], cw2).then_inc(S["signs2_loaded"], 16)
            e.wait_ge(S["y1_stored"], 16 * nb + 16)
            e.wait_ge(S["x3_stored"], 16 * nb + 16)
            for i in range(2):
                e.dma_start(arena[:, i * PIX:(i + 1) * PIX], y1_dram[i]).then_inc(S[f"b_loaded{i}"], 16)
            half = nb // 2

            def store_b(t, i):
                e.wait_ge(S["b_kept"], t * 2 * NWIN + (i + 2) * NWIN)
                e.dma_start(y2_dram[bass.ds(t * 2 + i, 1)].rearrange("a p n -> (a p) n"),
                            arena[:, (2 + i) * PIX:(3 + i) * PIX]).then_inc(S[f"b_stored{i}"], 16)

            def load_b(t, i):
                e.wait_ge(S["b_lo"], t * 2 * NWIN + (i + 1) * NWIN)
                e.dma_start(arena[:, i * PIX:(i + 1) * PIX],
                            y1_dram[bass.ds(t * 2 + i + 2, 1)].rearrange("a p n -> (a p) n")
                            ).then_inc(S[f"b_loaded{i}"], 16)
            if half > 1:
                with e.Fori(0, half - 1) as t:
                    for i in range(2):
                        load_b(t, i)
                        store_b(t, i)
            for i in range(2):
                store_b(half - 1, i)

            for i in range(2):
                e.wait_ge(S[f"b_stored{i}"], 16 * half + 16)
            e.wait_ge(S["b_stats"], NWIN * nb + 2 * NWIN)

            def load_c(t, i):
                e.dma_start(arena[:, 2 * i * PIX:(2 * i + 1) * PIX],
                            y2_dram[bass.ds(t * 2 + i, 1)].rearrange("a p n -> (a p) n")).then_inc(S[f"c_loaded{i}"], 16)
                e.dma_start(arena[:, (2 * i + 1) * PIX:(2 * i + 2) * PIX],
                            x3_dram[bass.ds(t * 2 + i, 1)].rearrange("a p n -> (a p) n")).then_inc(S[f"c_loaded{i}"], 16)

            def store_c(t, i):
                e.wait_ge(S["c_relu"], t * 2 + i + 1)
                e.dma_start(out[bass.ds(t * 2 + i, 1)].rearrange("a p n -> (a p) n"),
                            arena[:, 2 * i * PIX:(2 * i + 1) * PIX]).then_inc(S[f"c_stored{i}"], 16)
            for i in range(2):
                load_c(0, i)
            if half > 1:
                with e.Fori(0, half - 1) as t:
                    for i in range(2):
                        store_c(t, i)
                        e.wait_ge(S[f"c_stored{i}"], 16 * t + 16)
                        load_c(t + 1, i)
            for i in range(2):
                store_c(half - 1, i)
            for i in range(2):
                e.wait_ge(S[f"c_stored{i}"], 16 * half)

        @block.tensor
        def _(e):
            e.wait_ge(S["setup_loaded"], 144)
            for c in range(3):
                e.matmul(ps[:, 0, c:c + 1], wqkv_sb[:, c * P:(c + 1) * P], v_("ln1_b"), start=True, stop=True)
            for c in range(HID):
                mm = e.matmul(ps[:, 0, 3 + c:4 + c], w1_sb[:, c * P:(c + 1) * P], v_("ln2_b"), start=True, stop=True)
            mm.then_inc(S["setup_pe"], 1)

            def layer_norm(b, n, src):
                lb, off = 2 * NWIN, n * NWIN
                for s in range(NWIN):
                    if s >= 3:
                        e.wait_ge(S["squares"], b * lb + off + s - 2)
                    mm = e.matmul(ps[:, 5 + s % 3, 0:STRIP], centre_sb[:, :], src[:, s * STRIP:(s + 1) * STRIP],
                                  start=True, stop=True)
                    mm.then_inc(S["centred"], 1)
                    if s:
                        var_cols(b, n, s - 1)
                var_cols(b, n, NWIN - 1)
                e.wait_ge(S["rstd"], b * 2 + n + 1)
                e.transpose(ps[0:NLT, 1, 0:LT], ln_small[:, 0, :], eye_sb[0:LT, 0:LT]).then_inc(S["rstd_turned"], 1)
                e.wait_ge(S["rstd_rows"], b * 2 + n + 1)
                for s in range(NWIN):
                    if s >= 2:
                        e.wait_ge(S["normed"], b * lb + off + s - 1)
                    for i in range(LPS):
                        k = LPS * s + i
                        mm = e.matmul(ps[:, 3 + s % 2, i * LT:(i + 1) * LT],
                                      eye_sb[0:NLT, k:k + 1].to_broadcast([NLT, P]), rstd_t[:, :],
                                      start=True, stop=True)
                    mm.then_inc(S["rstd_spread"], 1)

            def var_cols(b, n, s):
                e.wait_ge(S["squares"], b * 2 * NWIN + n * NWIN + s + 1)
                for i in range(LPS):
                    k = LPS * s + i
                    mm = e.matmul(ps[0:LT, 2, k:k + 1], sq[:, s % 2, i * LT:(i + 1) * LT], mean_col[:, :],
                                  start=True, stop=True)
                mm.then_inc(S["variances"], 1)

            def q_project(b, r):
                e.matmul(ps[:, 5, 0:STRIP], wqkv_sb[:, 0:P],
                         xhat[:, bass.ds(r * STRIP, STRIP)], start=True, stop=True).then_inc(S["q_made"], 1)

            regs = [e.alloc_register(f"pe_key{i}") for i in range(TOPK)]

            def scores(b, w, half, j, queries=None):
                e.load(regs, key_off[0:1, bass.ds(w * TOPK, TOPK)])
                at = [e.snap(r, min_val=0, max_val=(NW - 1) * WPIX) for r in regs]
                if queries is not None:
                    e.wait_ge(S["q_kept"], queries)
                for p in range(2):
                    for i in range(TOPK):
                        mm = e.matmul(ps[:, (half * NWIN + j) % 2, p * KEYS + i * WPIX:p * KEYS + (i + 1) * WPIX],
                                      q_sb[:, half, j, 2 * p:2 * p + 2, :].rearrange("p h q -> p (h q)"),
                                      k_sb[:, bass.ds(at[i], WPIX)], start=True, stop=True)
                mm.then_inc(S["scores_made"], 1)

            def image(b, last):
                e.wait_ge(S["pos_done"], b * 9 + 9)
                layer_norm(b, 0, x1)
                e.wait_ge(S["normed"], b * 2 * NWIN + NWIN)
                for s in range(NWIN):
                    xs = xhat[:, s * STRIP:(s + 1) * STRIP]
                    if s:
                        e.wait_ge(S["k_kept"], b * NWIN + s)
                    e.matmul(ps[:, 6, 0:STRIP], wqkv_sb[:, P:2 * P], xs, start=True, stop=True).then_inc(S["k_made"], 1)
                    if s:
                        e.wait_ge(S["v_kept"], b * NWIN + s)
                    e.matmul(ps[:, 7, 0:STRIP], wqkv_sb[:, 2 * P:3 * P], xs, start=True, stop=True).then_inc(S["v_made"], 1)
                    if s:
                        e.wait_ge(S["vt_kept"], b * 2 * NWIN + 2 * s)
                    for j in range(NWIN):
                        w = xhat[:, s * STRIP + j * WPIX:s * STRIP + (j + 1) * WPIX]
                        for o in (0, WPIX):
                            mm = e.matmul(ps[o:o + WPIX, j // 4, (j % 4) * P:(j % 4 + 1) * P], w,
                                          wqkv_sb[:, 2 * P:3 * P], start=True, stop=True)
                    mm.then_inc(S["vt_made"], 1)
                e.wait_ge(S["win_sums"], b + 1)
                e.matmul(ps[:, 2, 0:NW], wqkv_sb[:, 0:P], win_sum[:, :], start=True, stop=True)
                e.matmul(ps[:, 2, NW:2 * NW], wqkv_sb[:, P:2 * P], win_sum[:, :], start=True,
                         stop=True).then_inc(S["win_qk_made"], 1)
                e.wait_ge(S["win_qk_kept"], b * 2 + 2)
                e.matmul(ps[0:NW, 2, 128:128 + NW], qk_win[:, 0, :], qk_win[:, 1, :], start=True,
                         stop=True).then_inc(S["logits_made"], 1)

                q_project(b, 0)
                e.wait_ge(S["k_kept"], b * NWIN + NWIN)
                e.wait_ge(S["vt_kept"], b * 2 * NWIN + 2 * NWIN)
                e.wait_ge(S["logits_kept"], b + 1)
                hold(e, S["offsets_placed"], b * 16 + 16)
                scores(b, 0, 0, 0, b * 4 * NWIN + 4)
                scores(b, 1, 0, 1)

                def step(r, half, j, tail):
                    n = b * NW + r * NWIN + j
                    slot = (half * NWIN + j) % 2
                    e.wait_ge(S["probs_scaled"], n * 2 + 2)
                    for p in range(2):
                        for f in range(2):
                            mm = e.transpose(ps[:, 2, (2 * p + f) * P:(2 * p + f + 1) * P],
                                             probs[:, slot, p, f * P:(f + 1) * P], eye_sb[:, :])
                    mm.then_inc(S["probs_turned"], 1)
                    if j == 2 and not tail:
                        e.wait_ge(S["q_kept"], b * 4 * NWIN + r * 4 + 4)
                        q_project(b, r + 1)
                    if j < NWIN - 2:
                        scores(b, r * NWIN + j + 2, half, j + 2)
                    elif not tail:
                        scores(b, r * NWIN + j + 2, 1 - half, j + 2 - NWIN,
                               b * 4 * NWIN + r * 4 + 8 if j == NWIN - 2 else None)
                    e.wait_ge(S["turned_kept"], n + 1)
                    e.wait_ge(S["v_chosen"], n * 4 + 4)
                    if j == 0:
                        e.wait_ge(S["mixed_kept"], b * NWIN + r + 1)
                    for f in range(2):
                        for h in range(HEADS):
                            mm = e.matmul(ps[HD * h:HD * h + HD, 3 + half, j * WPIX:(j + 1) * WPIX],
                                          vsel[:, slot, f, HD * h:HD * h + HD],
                                          probs_t[:, (2 * (h // 2) + f) * P + (h % 2) * WPIX:
                                                  (2 * (h // 2) + f) * P + (h % 2 + 1) * WPIX],
                                          start=(f == 0), stop=(f == 1))
                    mm.then_inc(S["mixed"], 1)
                window_rows(e, step)

                def lepe(s):
                    if s == 0:
                        e.wait_ge(S["v_kept"], b * NWIN + NWIN)
                    e.wait_ge(S[f"shifted{s % 2}"], (b * SLOT_STRIPS[s % 2] + s // 2 + 1) * ns)
                    if s >= 2:
                        e.wait_ge(S["lepe_kept"], b * NWIN + s - 1)
                    for t, (ty, tx) in enumerate(PLACES):
                        for g in range(HEADS):
                            src = shifted[:, s % 2, g, :].rearrange("p (h w) -> p h w", w=VW)
                            mm = e.matmul(ps[HD * g:HD * g + HD, 6 + s % 2, 0:STRIP],
                                          lepe_sb[:, g * NP + t, :], src[:, ty:ty + WIN, tx:tx + W],
                                          start=(t == 0), stop=(t == NP - 1))
                    mm.then_inc(S["lepe_made"], 1)

                lepe(0)
                e.wait_ge(S["mixed_kept"], b * NWIN + NWIN + 2)
                for s in range(NWIN):
                    if s + 1 < NWIN:
                        lepe(s + 1)
                    if s >= 2:
                        e.wait_ge(S["x2_done"], b * NWIN + s - 1)
                    e.wait_ge(S["lepe_kept"], b * NWIN + s + 1)
                    e.matmul(ps[:, s % 2, 0:STRIP], wo_sb[:, :], win(xc, s), start=True, stop=False)
                    e.matmul(ps[:, s % 2, 0:STRIP], wo_sb[:, :], lp[:, s % 2, :], start=False,
                             stop=True).then_inc(S["projected"], 1)
                e.wait_ge(S["x2_done"], b * NWIN + NWIN)
                layer_norm(b, 1, x2)

                def hidden(s):
                    if s == 0:
                        e.wait_ge(S["normed"], b * 2 * NWIN + 2 * NWIN)
                    else:
                        e.wait_ge(S["hidden_kept"], b * 3 * NWIN + 3 * s)
                    for c in range(HID):
                        e.matmul(ps[:, 5 + c, 0:STRIP], w1_sb[:, c * P:(c + 1) * P],
                                 xhat[:, s * STRIP:(s + 1) * STRIP], start=True, stop=True).then_inc(S["hidden_made"], 1)
                hidden(0)
                for s in range(NWIN):
                    if s + 1 < NWIN:
                        hidden(s + 1)
                    e.wait_ge(S["hidden_kept"], b * 3 * NWIN + 3 * s + 3)
                    if s >= 2:
                        e.wait_ge(S["x3_done"], b * NWIN + s - 1)
                    for c in range(HID):
                        mm = e.matmul(ps[:, s % 2, 0:STRIP], w2_sb[:, c, :], hid[:, s % 2, c, :],
                                      start=(c == 0), stop=(c == HID - 1))
                    mm.then_inc(S["mlp_made"], 1)

                binary_conv(b, cw_sign, S["hi_done"], S["lo_done"], S["conv_kept"], S["conv_made"], False,
                            lambda s: 3 + s % 2)

            def binary_conv(b, signs, hi_done, lo_done, kept, made, credits, bank):
                for s in range(NWIN):
                    have = min(s + 2, NWIN)
                    e.wait_ge(hi_done, b * NWIN + have)
                    e.wait_ge(lo_done, b * NWIN + have)
                    if credits:
                        e.wait_ge(kept, b * NWIN + s + 1)
                    elif s >= 2:
                        e.wait_ge(kept, b * NWIN + s - 1)
                    for t, (dy, dx) in enumerate(TAPS3):
                        for part in (hi, lo):
                            src = part[:, :].rearrange("p (h w) -> p h w", w=CW)
                            mm = e.matmul(ps[:, bank(s), 0:STRIP], signs[:, t, :],
                                          src[:, WIN * s + 1 + dy:WIN * s + 1 + dy + WIN, 1 + dx:1 + dx + W],
                                          start=(t == 0 and part is hi), stop=(t == 8 and part is lo))
                    mm.then_inc(made, 1)

            image_loop(e, image)

            e.sem_inc(S["b_made"], NWIN)
            e.wait_ge(S["setup_dve"], 12)
            with e.Fori(0, nb) as b:
                binary_conv(b, cw_sign, S["b_hi"], S["b_lo"], S["b_kept"], S["b_made"], True, lambda s: s)

        @block.scalar
        def _(e):
            e.sem_inc(S["b_kept"], NWIN)

            def layer_norm(b, n):
                lb, off = 2 * NWIN, n * NWIN
                if n == 0:
                    e.wait_ge(S["y1_stored"], b * 16 + 16)
                    e.wait_ge(S["conv_stats"], b * NWIN + NWIN)
                for s in range(NWIN):
                    e.wait_ge(S["centred"], b * lb + off + s + 1)
                    e.activation(xc[:, s * STRIP:(s + 1) * STRIP], ps[:, 5 + s % 3, 0:STRIP], ACT.Copy
                                 ).then_inc(S["centred_copied"], 1)
                    if s >= 2:
                        e.wait_ge(S["variances"], b * lb + off + s - 1)
                    e.activation(sq[:, s % 2, :], ps[:, 5 + s % 3, 0:STRIP], ACT.Square).then_inc(S["squares"], 1)
                e.wait_ge(S["eps_added"], b * 2 + n + 1)
                e.activation(ln_small[:, 1, :], ln_small[:, 0, :], ACT.Sqrt).then_inc(S["roots"], 1)

            def q_keep(b, half):
                for h in range(HEADS):
                    e.activation(q_sb[HD * h:HD * h + HD, half, :, h, :],
                                 ps[HD * h:HD * h + HD, 5, 0:STRIP].rearrange("p (j q) -> p j q", q=WPIX),
                                 ACT.Identity, bias=bq[HD * h:HD * h + HD, :], scale=SCALE).then_inc(S["q_kept"], 1)

            def exp(n, slot):
                e.wait_ge(S["max_found"], n + 1)
                for p in range(2):
                    e.activation(probs[:, slot, p, :], ps[:, slot, p * KEYS:(p + 1) * KEYS], ACT.Exp,
                                 bias=neg_max[:, slot, p:p + 1],
                                 accum_out=row_sum[:, slot, p:p + 1]).then_inc(S["exp_done"], 1)

            def image(b, last):
                layer_norm(b, 0)
                for s in range(NWIN):
                    e.wait_ge(S["k_made"], b * NWIN + s + 1)
                    e.activation(k_sb[:, s * STRIP:(s + 1) * STRIP], ps[:, 6, 0:STRIP], ACT.Identity,
                                 bias=bk).then_inc(S["k_kept"], 1)
                    e.wait_ge(S["v_made"], b * NWIN + s + 1)
                    dst = vpad[:, :].rearrange("p (h w) -> p h w", w=VW)[:, 2 + WIN * s:2 + WIN * (s + 1), 2:2 + W]
                    e.activation(dst.rearrange("p r (x c) -> p r x c", c=WIN),
                                 ps[:, 7, 0:STRIP].rearrange("p (x r c) -> p r x c", r=WIN, c=WIN), ACT.Identity,
                                 bias=bv).then_inc(S["v_kept"], 1)
                e.wait_ge(S["q_made"], b * NWIN + 1)
                q_keep(b, 0)
                exp(b * NW, 0)
                exp(b * NW + 1, 1)

                def step(r, half, j, tail):
                    n = b * NW + r * NWIN + j
                    slot = (half * NWIN + j) % 2
                    e.wait_ge(S["probs_turned"], n + 1)
                    e.activation(probs_t[:, :], ps[:, 2, :], ACT.Copy).then_inc(S["turned_kept"], 1)
                    if j == 2 and not tail:
                        e.wait_ge(S["q_made"], b * NWIN + r + 2)
                        q_keep(b, 1 - half)
                    if j < NWIN - 2 or not tail:
                        exp(n + 2, slot)
                window_rows(e, step)

                for s in range(NWIN):
                    e.wait_ge(S["lepe_made"], b * NWIN + s + 1)
                    if s >= 2:
                        e.wait_ge(S["projected"], b * NWIN + s - 1)
                    e.activation(lp[:, s % 2, :], ps[:, 6 + s % 2, 0:STRIP], ACT.Identity,
                                 bias=b_lepe).then_inc(S["lepe_kept"], 1)
                layer_norm(b, 1)
                for s in range(NWIN + 1):
                    if s < NWIN:
                        if s >= 2:
                            e.wait_ge(S["mlp_made"], b * NWIN + s - 1)
                        for c in range(HID):
                            e.wait_ge(S["hidden_made"], b * 3 * NWIN + 3 * s + c + 1)
                            e.activation(hid[:, s % 2, c, :], ps[:, 5 + c, 0:STRIP], ACT.Gelu,
                                         bias=bh[c]).then_inc(S["hidden_kept"], 1)
                    if s >= 1:
                        e.wait_ge(S["x3_done"], b * NWIN + s)
                        e.activation(inner(hi, s - 1), rows(x2, s - 1), ACT.Copy).then_inc(S["hi_done"], 1)
                for s in range(NWIN):
                    e.wait_ge(S["conv_made"], b * NWIN + s + 1)
                    e.activation(xc[:, s * STRIP:(s + 1) * STRIP], ps[:, 3 + s % 2, 0:STRIP],
                                 ACT.Copy).then_inc(S["conv_kept"], 1)

            image_loop(e, image)

            def bn_root(k):
                e.wait_ge(S["bn_dve"], k * 10 + 2)
                e.activation(bn_sb[:, 2:3], bn_sb[:, 1:2], ACT.Sqrt).then_inc(S["bn_act"], 1)

            bn_root(0)
            e.wait_ge(S["bn_dve"], 6)

            def part_b(t, i):
                b = t * 2 + i
                yin, yout = arena[:, i * PIX:(i + 1) * PIX], arena[:, (2 + i) * PIX:(3 + i) * PIX]
                e.wait_ge(S[f"b_loaded{i}"], 16 * t + 16)
                e.wait_ge(S[f"b_stored{i}"], 16 * t + 16)
                e.wait_ge(S["b_stats"], t * 2 * NWIN + 2 * NWIN)
                for s in range(NWIN + 2):
                    if s < NWIN:
                        e.wait_ge(S["b_made"], b * NWIN + min(s + 2, NWIN))
                        ys = yin[:, s * STRIP:(s + 1) * STRIP]
                        e.activation(ys, ys, ACT.Relu, bias=bn_sb[:, 5:6], scale=bn_sb[:, 4:5]).then_inc(S["relu_done"], 1)
                        e.wait_ge(S["relu_done"], b * NWIN + s + 1)
                        e.activation(inner(hi, s), rows(yin, s), ACT.Copy).then_inc(S["b_hi"], 1)
                    if s >= 2:
                        e.wait_ge(S["b_made"], b * NWIN + NWIN + s - 1)
                        e.activation(yout[:, (s - 2) * STRIP:(s - 1) * STRIP], ps[:, s - 2, 0:STRIP],
                                     ACT.Copy).then_inc(S["b_kept"], 1)
            with e.Fori(0, nb // 2) as t:
                part_b(t, 0)
                part_b(t, 1)
            bn_root(1)
            e.wait_ge(S["bn_dve"], 16)
            with e.Fori(0, nb // 2) as t:
                for i in range(2):
                    e.wait_ge(S["c_sum"], t * 2 + i + 1)
                    u = arena[:, 2 * i * PIX:(2 * i + 1) * PIX]
                    e.activation(u, u, ACT.Relu, bias=bn_sb[:, 5:6]).then_inc(S["c_relu"], 1)

        @block.gpsimd
        def _(e):
            e.memset(q_sb[:, :, :, :, :], 0.0).then_inc(S["pad_zero"], 1)
            e.memset(vpad[:, :], 0.0).then_inc(S["pad_zero"], 1)
            e.memset(hi[:, :].bitcast(F32), 0.0).then_inc(S["pad_zero"], 1)
            e.memset(lo[:, :].bitcast(F32), 0.0).then_inc(S["pad_zero"], 1)
            e.memset(mean_col[:, :], 1.0 / P).then_inc(S["pad_zero"], 1)
            regs = [e.alloc_register(f"pool_key{i}") for i in range(TOPK)]

            def choose(b, r, slot, j):
                w = r * NWIN + j
                n = b * NW + w
                e.load(regs, key_off[0:1, bass.ds(w * TOPK, TOPK)])
                at = [e.snap(q, min_val=0, max_val=(NW - 1) * WPIX) for q in regs]
                hold(e, S["mixed"], n + 1)
                for i in range(TOPK):
                    o = WPIX * (i % 2)
                    e.tensor_copy(vsel[o:o + WPIX, slot, i // 2, :],
                                  vt[o:o + WPIX, bass.ds(at[i] * 2, P)]).then_inc(S["v_chosen"], 1)

            def image(b, last):
                e.wait_ge(S["offsets_placed"], b * 16 + 16)
                hold(e, S["vt_kept"], b * 2 * NWIN + 2 * NWIN)
                window_rows(e, lambda r, half, j, tail: choose(b, r, (half * NWIN + j) % 2, j))
            e.sem_inc(S["mixed"], 2)
            image_loop(e, image)

        @block.vector
        def _(e):
            e.wait_ge(S["setup_loaded"], 144)
            e.wait_ge(S["setup_pe"], 1)
            e.wait_ge(S["pad_zero"], 5)
            n_setup = [0]

            def mark(ins):
                n_setup[0] += 1
                ins.then_inc(S["setup_dve"], 1)

            mark(e.tensor_tensor(bias[:, 0:3], ps[:, 0, 0:3], vec_sb[:, VEC["qkv_b"]:VEC["qkv_b"] + 3], ALU.add))
            mark(e.tensor_tensor(bias[:, 3:6], ps[:, 0, 3:6], vec_sb[:, VEC["mlp_b1"]:VEC["mlp_b1"] + 3], ALU.add))
            mark(e.tensor_scalar(wqkv_sb[:, :], wqkv_sb[:, :], v_("ln1_g"), None, ALU.mult))
            mark(e.tensor_scalar(w1_sb[:, :], w1_sb[:, :], v_("ln2_g"), None, ALU.mult))
            mark(e.tensor_scalar(pos_centre, v_("pos_w", 4), 1.0, None, ALU.add))
            mark(e.tensor_tensor(lepe_sb[:, :, :], eye4_sb[:, :].unsqueeze(1).to_broadcast([P, HEADS * NP, HD]),
                                 vec_sb[:, VEC["lepe_taps"]:VEC["lepe_taps"] + HEADS * NP].unsqueeze(2)
                                 .to_broadcast([P, HEADS * NP, HD]), ALU.mult))
            def signs():
                negative, raw = k_sb[:, 0:9 * P], xhat[:, 0:9 * P]
                mark(e.tensor_scalar(negative, raw, 0.0, None, ALU.is_lt))
                e.wait_ge(S["setup_dve"], n_setup[0])
                mark(e.scalar_tensor_tensor(out=cw_sign[:, :, :].rearrange("p t c -> p (t c)"), in0=raw,
                                            scalar=0.0, in1=negative, op0=ALU.is_gt, op1=ALU.subtract))
            signs()
            e.wait_ge(S["setup_dve"], n_setup[0])
            mark(e.tensor_tensor(b_lepe, v_("lepe_b"), bv, ALU.add))
            mark(e.tensor_scalar(bq, bq, SCALE, None, ALU.mult))
            e.wait_ge(S["setup_dve"], n_setup[0])
            e.sem_inc(S["mixed_kept"], 2)
            e.sem_inc(S["conv_stats"], NWIN)
            e.sem_inc(S["b_stats"], 2 * NWIN)

            order = [4, 0, 1, 2, 3, 5, 6, 7, 8]

            def pos_tap(base, k):
                t = order[k]
                dy, dx = TAPS3[t]
                if k == 0:
                    e.tensor_scalar(x1, xin, pos_centre, v_("pos_b"), ALU.mult, ALU.add).then_inc(S["pos_done"], 1)
                    return
                a, i = (z.rearrange("p (h w) -> p h w", w=W) for z in (x1, xin))
                y0, y1 = max(0, -dy), H - max(0, dy)
                c0, c1 = max(0, -dx), W - max(0, dx)
                e.wait_ge(S["pos_done"], base + k)
                acc = a[:, y0:y1, c0:c1]
                e.scalar_tensor_tensor(out=acc, in0=i[:, y0 + dy:y1 + dy, c0 + dx:c1 + dx], scalar=v_("pos_w", t),
                                       in1=acc, op0=ALU.mult, op1=ALU.add).then_inc(S["pos_done"], 1)

            def layer_norm(b, n, put):
                lb, off = 2 * NWIN, n * NWIN
                e.wait_ge(S["variances"], b * lb + off + NWIN)
                e.tensor_scalar(ln_small[:, 0, :], ps[0:LT, 2, 0:NLT], LN_EPS, None, ALU.add).then_inc(S["eps_added"], 1)
                e.wait_ge(S["roots"], b * 2 + n + 1)
                e.reciprocal(ln_small[:, 0, :], ln_small[:, 1, :]).then_inc(S["rstd"], 1)
                e.wait_ge(S["rstd_turned"], b * 2 + n + 1)
                e.tensor_copy(rstd_t[:, :], ps[0:NLT, 1, 0:LT]).then_inc(S["rstd_rows"], 1)
                e.wait_ge(S["centred_copied"], b * lb + off + NWIN)
                for s in range(NWIN):
                    e.wait_ge(S["rstd_spread"], b * lb + off + s + 1)
                    e.tensor_tensor(put(xhat, s), img(xc, s),
                                    ps[:, 3 + s % 2, 0:STRIP].rearrange("p (r x c) -> p r x c", r=WIN, c=WIN),
                                    ALU.mult).then_inc(S["normed"], 1)

            def row_max(n, slot):
                e.wait_ge(S["scores_made"], n + 1)
                e.tensor_reduce(neg_max[:, slot, :], ps[:, slot, :].rearrange("p (a k) -> p a k", a=2), AX.X,
                                ALU.max, negate=True).then_inc(S["max_found"], 1)

            def scale_probs(n, slot):
                e.wait_ge(S["exp_done"], n * 2 + 2)
                e.reciprocal(row_inv[:, slot, :], row_sum[:, slot, :]).then_inc(S["inv_done"], 1)
                e.wait_ge(S["inv_done"], n + 1)
                for p in range(2):
                    e.tensor_scalar(probs[:, slot, p, :], probs[:, slot, p, :], row_inv[:, slot, p:p + 1], None,
                                    ALU.mult).then_inc(S["probs_scaled"], 1)

            for k in range(9):
                if k == 0:
                    e.wait_ge(S["x_loaded"], 16)
                pos_tap(0, k)

            def image(b, last):
                layer_norm(b, 0, win)
                for s in range(NWIN):
                    e.wait_ge(S["vt_made"], b * NWIN + s + 1)
                    e.tensor_copy(vt[:, s * NWIN * P:(s * NWIN + 4) * P], ps[:, 0, :]).then_inc(S["vt_kept"], 1)
                    e.tensor_copy(vt[:, (s * NWIN + 4) * P:(s + 1) * NWIN * P], ps[:, 1, 0:3 * P]
                                  ).then_inc(S["vt_kept"], 1)
                    if s == 0:
                        e.wait_ge(S["normed"], b * 2 * NWIN + NWIN)
                        e.tensor_reduce(win_sum[:, :], xhat.rearrange("p (w q) -> p w q", q=WPIX), AX.X,
                                        ALU.add).then_inc(S["win_sums"], 1)
                e.wait_ge(S["win_qk_made"], b + 1)
                e.tensor_scalar(qk_win[:, 0, :], ps[:, 2, 0:NW], SCALE / WPIX, bq, ALU.mult,
                                ALU.add).then_inc(S["win_qk_kept"], 1)
                e.tensor_scalar(qk_win[:, 1, :], ps[:, 2, NW:2 * NW], 1.0 / WPIX, bk, ALU.mult,
                                ALU.add).then_inc(S["win_qk_kept"], 1)
                e.wait_ge(S["logits_made"], b + 1)
                e.tensor_copy(logits[:, :], ps[0:NW, 2, 128:128 + NW]).then_inc(S["logits_kept"], 1)
                hold(e, S["logits_kept"], b + 1)
                e.max(top8[:, :], logits[:, :]).then_inc(S["top_values"], 1)
                hold(e, S["top_values"], b + 1)
                e.max_index(top_i[:, :], top8[:, :], logits[:, :]).then_inc(S["top_found"], 1)
                e.wait_ge(S["top_found"], b + 1)
                e.tensor_scalar(top_off[:, :], top_i[:, 0:TOPK], float(WPIX), None, ALU.mult).then_inc(S["offsets"], 1)

                row_max(b * NW, 0)
                row_max(b * NW + 1, 1)
                scale_probs(b * NW, 0)

                def step(r, half, j, tail):
                    n = b * NW + r * NWIN + j
                    slot = (half * NWIN + j) % 2
                    if j < NWIN - 2 or not tail:
                        row_max(n + 2, slot)
                    if j < NWIN - 1 or not tail:
                        scale_probs(n + 1, 1 - slot)
                    if j == NWIN - 1:
                        e.wait_ge(S["mixed"], n + 3)
                        e.tensor_copy(xc[:, bass.ds(r * STRIP, STRIP)], ps[:, 3 + half, 0:STRIP]
                                      ).then_inc(S["mixed_kept"], 1)
                window_rows(e, step)

                e.wait_ge(S["x3_stored"], b * 16 + 16)
                for s in range(NWIN):
                    e.wait_ge(S["projected"], b * NWIN + s + 1)
                    e.scalar_tensor_tensor(out=x2[:, s * STRIP:(s + 1) * STRIP], in0=ps[:, s % 2, 0:STRIP],
                                           scalar=v_("wo_b"), in1=x1[:, s * STRIP:(s + 1) * STRIP], op0=ALU.add,
                                           op1=ALU.add).then_inc(S["x2_done"], 1)
                layer_norm(b, 1, img)
                for s in range(NWIN):
                    e.wait_ge(S["mlp_made"], b * NWIN + s + 1)
                    xs = x2[:, s * STRIP:(s + 1) * STRIP]
                    e.scalar_tensor_tensor(out=xs, in0=ps[:, s % 2, 0:STRIP], scalar=v_("mlp_b2"), in1=xs,
                                           op0=ALU.add, op1=ALU.add).then_inc(S["x3_done"], 1)
                    if not last:
                        if s == 0:
                            e.wait_ge(S["x_loaded"], b * 16 + 32)
                        pos_tap(b * 9 + 9, s)
                    e.wait_ge(S["hi_done"], b * NWIN + s + 1)
                    e.tensor_tensor(inner(lo, s), rows(x2, s), inner(hi, s).bitcast(F32),
                                    ALU.subtract).then_inc(S["lo_done"], 1)
                for s in range(NWIN):
                    e.wait_ge(S["conv_kept"], b * NWIN + s + 1)
                    e.bn_stats(stats[:, bass.ds(b * NWIN + s, 1), :].rearrange("p a k -> p (a k)"),
                               xc[:, s * STRIP:(s + 1) * STRIP]).then_inc(S["conv_stats"], 1)
                    if not last and s in (0, 1):
                        pos_tap(b * 9 + 9, NWIN + s)

            image_loop(e, image)

            def batch_norm(k, counted, credits, gamma, beta):
                def m(ins, n):
                    ins.then_inc(S["bn_dve"], n)
                e.wait_ge(counted, nb * NWIN + credits)
                m(e.bn_aggr(bn_sb[:, 0:2], stats[:, :, :].rearrange("p a k -> p (a k)")), 1)
                e.wait_ge(S["bn_dve"], k * 10 + 1)
                m(e.tensor_scalar(bn_sb[:, 1:2], bn_sb[:, 1:2], BN_EPS, None, ALU.add), 1)
                e.wait_ge(S["bn_act"], k + 1)
                m(e.reciprocal(bn_sb[:, 3:4], bn_sb[:, 2:3]), 1)
                e.wait_ge(S["bn_dve"], k * 10 + 3)
                if k:
                    e.wait_ge(S["relu_done"], nb * NWIN)
                m(e.tensor_tensor(bn_sb[:, 4:5], bn_sb[:, 3:4], gamma, ALU.mult), 1)
                e.wait_ge(S["bn_dve"], k * 10 + 4)
                m(e.tensor_tensor(bn_sb[:, 2:3], bn_sb[:, 0:1], bn_sb[:, 4:5], ALU.mult), 1)
                e.wait_ge(S["bn_dve"], k * 10 + 5)
                m(e.tensor_tensor(bn_sb[:, 5:6], beta, bn_sb[:, 2:3], ALU.subtract), 5)

            batch_norm(0, S["conv_stats"], NWIN, v_("gamma1"), v_("beta1"))
            e.wait_ge(S["signs2_loaded"], 16)
            signs()

            def part_b(t, i):
                b = t * 2 + i
                yin = arena[:, i * PIX:(i + 1) * PIX]
                for s in range(NWIN + 2):
                    if s < NWIN:
                        e.wait_ge(S["b_hi"], b * NWIN + s + 1)
                        e.tensor_tensor(inner(lo, s), rows(yin, s), inner(hi, s).bitcast(F32),
                                        ALU.subtract).then_inc(S["b_lo"], 1)
                    if s >= 2:
                        e.wait_ge(S["b_kept"], b * NWIN + NWIN + s - 1)
                        e.bn_stats(stats[:, bass.ds(b * NWIN + s - 2, 1), :].rearrange("p a k -> p (a k)"),
                                   arena[:, (2 + i) * PIX + (s - 2) * STRIP:(2 + i) * PIX + (s - 1) * STRIP]).then_inc(S["b_stats"], 1)
            e.wait_ge(S["bn_dve"], 10)
            with e.Fori(0, nb // 2) as t:
                part_b(t, 0)
                part_b(t, 1)
            batch_norm(1, S["b_stats"], 2 * NWIN, v_("gamma2"), v_("beta2"))
            e.wait_ge(S["bn_dve"], 20)
            with e.Fori(0, nb // 2) as t:
                for i in range(2):
                    e.wait_ge(S[f"c_loaded{i}"], 32 * t + 32)
                    u = arena[:, 2 * i * PIX:(2 * i + 1) * PIX]
                    e.scalar_tensor_tensor(out=u, in0=u, scalar=bn_sb[:, 4:5],
                                           in1=arena[:, (2 * i + 1) * PIX:(2 * i + 2) * PIX], op0=ALU.mult,
                                           op1=ALU.add).then_inc(S["c_sum"], 1)


def lay_out(inputs, nb):
    f = {k: np.asarray(v) for k, v in inputs.items()}
    vec = np.zeros((P, NVEC), np.float32)

    def put(name, a, k=1):
        vec[:, VEC[name]:VEC[name] + k] = a

    L0 = "L0_conv_"
    put("pos_w", f[L0 + "pos_w"].reshape(P, 9), 9)
    for name in ("pos_b", "ln1_g", "ln1_b", "lepe_b", "wo_b", "ln2_g", "ln2_b", "mlp_b2"):
        put(name, f[L0 + name].reshape(P, 1))
    put("qkv_b", f[L0 + "qkv_b"].reshape(3, P).T, 3)
    put("mlp_b1", f[L0 + "mlp_b1"].reshape(HID, P).T, HID)
    for name in ("gamma1", "beta1", "gamma2", "beta2"):
        put(name, f["L1_conv_" + name].reshape(P, 1))
    lepe = f[L0 + "lepe_w"].reshape(P, 5, 5)
    for t, row in enumerate(lepe_cover()):
        for k, tap in enumerate(row):
            for g in range(HEADS):
                if tap is not None:
                    vec[HD * k:HD * k + HD, VEC["lepe_taps"] + g * NP + t] = lepe[HD * g:HD * g + HD, tap[0], tap[1]]

    def conv(w):
        return np.ascontiguousarray(w.transpose(1, 2, 3, 0).reshape(P, 9 * P))

    eye = np.eye(P, dtype=np.float32)
    return {
        "x": np.ascontiguousarray(f["x"].reshape(-1, P, PIX)[:nb]),
        "vec": vec,
        "wqkv": f[L0 + "qkv_w"], "wo": f[L0 + "wo_w"], "w1": f[L0 + "mlp_w1"], "w2": f[L0 + "mlp_w2"],
        "cw1": conv(f["L1_conv_w1"]), "cw2": conv(f["L1_conv_w2"]),
        "eye": eye, "centre": eye - np.float32(1.0 / P), "eye4": np.tile(eye[0:HD, 0:HD], (4, 1)),
    }


def kernel(**inputs):
    import concourse.bacc as _bacc
    from concourse.bass_utils import run_bass_kernel_spmd as _run

    nb = inputs["x"].shape[0]
    arrays = lay_out(inputs, nb)
    nc = _bacc.Bacc("TRN2", target_bir_lowering=False, num_devices=1)
    aps = {n: nc.dram_tensor(n, a.shape, F32, kind="ExternalInput").ap() for n, a in arrays.items()}
    out = nc.dram_tensor("out", (nb, P, PIX), F32, kind="ExternalOutput").ap()
    build(nc, **aps, out=out, nb=nb)
    r = _run(nc, [arrays], core_ids=[0])
    return r.results[0]["out"].reshape(nb, P, H, W)
```

```python
from contextlib import ExitStack

import numpy as np

import concourse.bass as bass
from concourse import mybir

F32 = mybir.dt.float32
F32R = mybir.dt.float32r
U32 = mybir.dt.uint32
ALU = mybir.AluOpType
ACT = mybir.ActivationFunctionType
AX = mybir.AxisListType

P = 128
H = W = 56
PIX = H * W
NWIN = 7
WIN = 8
WPIX = WIN * WIN
NW = NWIN * NWIN
STRIP = WIN * W
HEADS, HD = 4, 32
TOPK = 4
KEYS = TOPK * WPIX
PAIR = 2 * WPIX
HID = 3
SCALE = float(P) ** -0.5
LN_EPS = 1e-6
BN_EPS = 1e-5
LT = 112
NLT = PIX // LT
LPS = STRIP // LT

SHIFTS = [(0, 0), (0, 2), (0, 3), (1, 0)]
PLACES = [(0, 0), (0, 1), (1, 0), (1, 2), (2, 1), (3, 0), (3, 2), (4, 1)]
NS, NP = len(SHIFTS), len(PLACES)
VW = W + 4
VROWS = H + 6
RLEN = (WIN + 4) * VW
CW = W + 2
TAPS3 = [(dy, dx) for dy in (-1, 0, 1) for dx in (-1, 0, 1)]

VEC = {}
_n = 0
for _name, _k in [("pos_w", 9), ("pos_b", 1), ("ln1_g", 1), ("ln1_b", 1), ("qkv_b", 3), ("lepe_b", 1),
                  ("wo_b", 1), ("ln2_g", 1), ("ln2_b", 1), ("mlp_b1", HID), ("mlp_b2", 1), ("gamma1", 1),
                  ("beta1", 1), ("gamma2", 1), ("beta2", 1), ("lepe_taps", HEADS * NP)]:
    VEC[_name] = _n
    _n += _k
NVEC = _n


def lepe_cover():
    taken, out = set(), []
    for ty, tx in PLACES:
        row = []
        for sy, sx in SHIFTS:
            tap = (ty + sy, tx + sx)
            new = tap[0] < 5 and tap[1] < 5 and tap not in taken
            if new:
                taken.add(tap)
            row.append(tap if new else None)
        out.append(row)
    assert len(taken) == 25
    return out


def build(nc, x, vec, wqkv, wo, w1, w2, cw1, cw2, eye, centre, eye4, out, nb, dump=None):
    x3_dram = nc.dram_tensor("x3_scratch", [nb, P, PIX], F32).ap()
    y1_dram = nc.dram_tensor("y1_scratch", [nb, P, PIX], F32).ap()
    y2_dram = nc.dram_tensor("y2_scratch", [nb, P, PIX], F32).ap()

    with ExitStack() as ctx:
        def sb(name, shape, dt=F32):
            return ctx.enter_context(nc.sbuf_tensor(name, shape, dt))

        def sem(name):
            return ctx.enter_context(nc.semaphore(name))

        ps = ctx.enter_context(nc.psum_tensor("ps", [P, 8, 512], F32))

        vec_sb = sb("vec_sb", [P, NVEC])
        eye_sb = sb("eye_sb", [P, P])
        centre_sb = sb("centre_sb", [P, P])
        eye4_sb = sb("eye4_sb", [P, HD])
        mean_col = sb("mean_col", [P, 1])
        spread_sb = sb("spread_sb", [2 * HD, NLT], F32R)
        wqkv_sb = sb("wqkv_sb", [P, 3 * P])
        wo_sb = sb("wo_sb", [P, P])
        w1_sb = sb("w1_sb", [P, HID * P])
        w2_sb = sb("w2_sb", [P, HID, P])
        cw_sign = sb("cw_sign", [P, 9, P], F32R)
        lepe_sb = sb("lepe_sb", [P, HEADS * NP, HD])
        bias = sb("bias", [P, 10])
        bq, bk, bv = (bias[:, i:i + 1] for i in range(3))
        bh = [bias[:, 3 + c:4 + c] for c in range(HID)]
        b_lepe = bias[:, 6:7]
        pos_centre = bias[:, 7:8]

        def v_(name, i=0):
            return vec_sb[:, VEC[name] + i:VEC[name] + i + 1]

        arena = sb("arena", [P, 6 * PIX])
        xin = arena[:, 0:PIX]
        x1 = arena[:, PIX:2 * PIX]
        x2 = arena[:, 2 * PIX:3 * PIX]
        xc = arena[:, 3 * PIX:4 * PIX]
        xhat = arena[:, 4 * PIX:5 * PIX]
        k_sb = arena[:, 5 * PIX:6 * PIX]
        q_sb = sb("q_sb", [P, 2, NWIN, HEADS, WPIX])
        vpad = sb("vpad", [P, VROWS * VW])
        shifted = sb("shifted", [P, 2, HEADS, RLEN])
        hid = shifted[:, :, 0:2, :].rearrange("p a g n -> p a (g n)")[:, :, 0:HID * STRIP].rearrange(
            "p a (c n) -> p a c n", c=HID)
        sq = hid[:, :, 0, :]
        vt = sb("vt", [P, NW * P])
        y1 = vt[:, 0:PIX]
        vsel = sb("vsel", [P, 2, 2, P])
        ksel = sb("ksel", [P, 2, KEYS])
        probs = sb("probs", [P, 2, 2, KEYS])
        probs_t = sb("probs_t", [P, 4 * P])
        neg_max = sb("neg_max", [P, 2, 2])
        row_sum = sb("row_sum", [P, 2, 2])
        row_inv = sb("row_inv", [P, 2, 2])
        ln_small = sb("ln_small", [LT, 2, NLT])
        rstd_parts = sb("rstd_parts", [LT, 2 * HD])
        rstd_t = sb("rstd_t", [2 * HD, LT], F32R)
        win_sum = sb("win_sum", [P, NW])
        qk_win = sb("qk_win", [P, 2, NW])
        logits = sb("logits", [NW, NW])
        top8 = sb("top8", [NW, 8])
        top_i = sb("top_i", [NW, 8], U32)
        top_off = sb("top_off", [NW, TOPK], U32)
        key_off = sb("key_off", [1, NW * TOPK], U32)
        hi = sb("hi", [P, CW * CW], F32R)
        lo = sb("lo", [P, CW * CW], F32R)
        stats = sb("stats", [P, nb * NWIN, 6])
        bn_sb = sb("bn_sb", [P, 6])

        def img(t, s):
            return t[:, s * STRIP:(s + 1) * STRIP].rearrange("p (r x c) -> p r x c", r=WIN, c=WIN)

        def win(t, s):
            return t[:, s * STRIP:(s + 1) * STRIP].rearrange("p (x r c) -> p r x c", r=WIN, c=WIN)

        def inner(t, s):
            return t[:, :].rearrange("p (h w) -> p h w", w=CW)[:, 1 + WIN * s:1 + WIN * (s + 1), 1:1 + W]

        def rows(t, s):
            return t[:, s * STRIP:(s + 1) * STRIP].rearrange("p (r w) -> p r w", w=W)

        S = {n: sem(n) for n in (
            "setup_loaded", "setup_dve", "setup_pe", "x_loaded", "pos_done",
            "centred", "centred_copied", "squares", "variances", "eps_added", "roots", "rstd", "rstd_high",
            "rstd_low", "rstd_turned", "k_chosen",
            "rstd_rows", "rstd_spread", "normed",
            "k_made", "v_made", "vt_made", "k_kept", "v_kept", "vt_kept",
            "win_sums", "win_qk_made", "win_qk_kept", "logits_made", "logits_kept", "top_values", "top_found",
            "offsets", "offsets_placed",
            "q_made", "q_kept", "scores_made", "max_found", "exp_done", "inv_done", "probs_scaled",
            "probs_turned", "turned_kept", "v_chosen", "mixed", "mixed_kept",
            "shifted0", "shifted1", "lepe_made", "lepe_kept", "projected", "x2_done",
            "hidden_made", "hidden_kept", "mlp_made", "x3_done", "hi_done", "lo_done",
            "conv_made", "conv_kept", "conv_stats", "x3_stored", "y1_stored",
            "b_loaded0", "b_loaded1", "relu_done", "b_hi", "b_lo", "b_made", "b_kept", "b_stats", "b_stored0",
            "b_stored1", "bn_dve", "bn_act", "c_loaded0", "c_loaded1", "c_sum", "c_relu", "c_stored0",
            "c_stored1", "pad_zero", "signs2_loaded", "held")}

        ns = len(SHIFTS) * HEADS * 16
        SLOT_STRIPS = (4, 3)

        block = ctx.enter_context(nc.Block())

        def hold(e, which, value):
            e.wait_ge(which, value)
            e.sem_inc(S["held"], 1)

        def image_loop(e, body):
            assert nb >= 2
            body(0, True, False)
            if nb > 2:
                with e.Fori(1, nb - 1) as b:
                    body(b, False, False)
            body(nb - 1, False, True)

        def window_rows(e, step):
            with e.Fori(0, NWIN // 2) as t:
                for half in range(2):
                    for j in range(NWIN):
                        step(t, half, j, False)
            for j in range(NWIN):
                step(NWIN // 2, 0, j, True)

        @block.sync
        def _(e):
            loads = [(vec_sb, vec), (eye_sb, eye), (centre_sb, centre), (eye4_sb, eye4), (wqkv_sb, wqkv),
                     (wo_sb, wo), (w1_sb, w1)]
            for dst, src in loads:
                e.dma_start(dst[:, :], src).then_inc(S["setup_loaded"], 16)
            e.dma_start(w2_sb[:, :, :], w2.rearrange("(c p) n -> p c n", p=P)).then_inc(S["setup_loaded"], 16)
            e.dma_start(xhat[:, 0:9 * P], cw1).then_inc(S["setup_loaded"], 16)
            e.dma_start(xin, x[0]).then_inc(S["x_loaded"], 16)

            def store_y1(b):
                e.wait_ge(S["conv_kept"], b * NWIN + NWIN)
                e.dma_start(y1_dram[bass.ds(b, 1)].rearrange("a p n -> (a p) n"), y1).then_inc(S["y1_stored"], 16)

            def image(b, first, last):
                if not last:
                    e.wait_ge(S["pos_done"], b * 9 + 9)
                    e.dma_start(xin, x[bass.ds(b + 1, 1)].rearrange("a p n -> (a p) n")).then_inc(S["x_loaded"], 16)
                if not first:
                    store_y1(b - 1)
                e.wait_ge(S["offsets"], b + 1)
                e.dma_start(key_off[0:1, :], top_off[:, :]).then_inc(S["offsets_placed"], 16)
                e.wait_ge(S["v_kept"], b * NWIN + NWIN)
                for s in range(NWIN):
                    if s >= 2:
                        e.wait_ge(S["lepe_made"], b * NWIN + s - 1)
                    for k, (sy, sx) in enumerate(SHIFTS):
                        for g in range(HEADS):
                            at = WIN * s * VW + sy * VW + sx
                            e.dma_start(shifted[HD * k:HD * k + HD, s % 2, g, :],
                                        vpad[HD * g:HD * g + HD, at:at + RLEN]).then_inc(S[f"shifted{s % 2}"], 16)
                e.wait_ge(S["x3_done"], b * NWIN + NWIN)
                e.dma_start(x3_dram[bass.ds(b, 1)].rearrange("a p n -> (a p) n"), x2).then_inc(S["x3_stored"], 16)

            for name in ("x3_stored", "b_stored0", "b_stored1"):
                e.sem_inc(S[name], 16)
            image_loop(e, image)
            store_y1(nb - 1)

            def part_b(b, i):
                yin, yout = arena[:, i * PIX:(i + 1) * PIX], arena[:, (2 + i) * PIX:(3 + i) * PIX]
                return yin, yout
            e.wait_ge(S["hidden_made"], 3 * NWIN * nb)
            e.dma_start(xhat[:, 0:9 * P], cw2).then_inc(S["signs2_loaded"], 16)
            e.wait_ge(S["y1_stored"], 16 * nb)
            e.wait_ge(S["x3_stored"], 16 * nb + 16)
            for i in range(2):
                e.dma_start(arena[:, i * PIX:(i + 1) * PIX], y1_dram[i]).then_inc(S[f"b_loaded{i}"], 16)
            half = nb // 2

            def store_b(t, i):
                e.wait_ge(S["b_kept"], t * 2 * NWIN + (i + 2) * NWIN)
                e.dma_start(y2_dram[bass.ds(t * 2 + i, 1)].rearrange("a p n -> (a p) n"),
                            arena[:, (2 + i) * PIX:(3 + i) * PIX]).then_inc(S[f"b_stored{i}"], 16)

            def load_b(t, i):
                e.wait_ge(S["b_lo"], t * 2 * NWIN + (i + 1) * NWIN)
                e.dma_start(arena[:, i * PIX:(i + 1) * PIX],
                            y1_dram[bass.ds(t * 2 + i + 2, 1)].rearrange("a p n -> (a p) n")
                            ).then_inc(S[f"b_loaded{i}"], 16)
            if half > 1:
                with e.Fori(0, half - 1) as t:
                    for i in range(2):
                        load_b(t, i)
                        store_b(t, i)
            for i in range(2):
                store_b(half - 1, i)

            for i in range(2):
                e.wait_ge(S[f"b_stored{i}"], 16 * half + 16)
            e.wait_ge(S["b_stats"], NWIN * nb + 2 * NWIN)

            def load_c(t, i):
                e.dma_start(arena[:, 2 * i * PIX:(2 * i + 1) * PIX],
                            y2_dram[bass.ds(t * 2 + i, 1)].rearrange("a p n -> (a p) n")).then_inc(S[f"c_loaded{i}"], 16)
                e.dma_start(arena[:, (2 * i + 1) * PIX:(2 * i + 2) * PIX],
                            x3_dram[bass.ds(t * 2 + i, 1)].rearrange("a p n -> (a p) n")).then_inc(S[f"c_loaded{i}"], 16)

            def store_c(t, i):
                e.wait_ge(S["c_relu"], t * 2 + i + 1)
                e.dma_start(out[bass.ds(t * 2 + i, 1)].rearrange("a p n -> (a p) n"),
                            arena[:, 2 * i * PIX:(2 * i + 1) * PIX]).then_inc(S[f"c_stored{i}"], 16)
            for i in range(2):
                load_c(0, i)
            if half > 1:
                with e.Fori(0, half - 1) as t:
                    for i in range(2):
                        store_c(t, i)
                        e.wait_ge(S[f"c_stored{i}"], 16 * t + 16)
                        load_c(t + 1, i)
            for i in range(2):
                store_c(half - 1, i)
            for i in range(2):
                e.wait_ge(S[f"c_stored{i}"], 16 * half)

        @block.tensor
        def _(e):
            e.wait_ge(S["setup_loaded"], 144)
            for c in range(3):
                e.matmul(ps[:, 0, c:c + 1], wqkv_sb[:, c * P:(c + 1) * P], v_("ln1_b"), start=True, stop=True)
            for c in range(HID):
                mm = e.matmul(ps[:, 0, 3 + c:4 + c], w1_sb[:, c * P:(c + 1) * P], v_("ln2_b"), start=True, stop=True)
            mm.then_inc(S["setup_pe"], 1)

            def centre(b, n, s, src):
                if s >= 3:
                    e.wait_ge(S["squares"], (b * 2 + n) * NWIN + s - 2)
                e.matmul(ps[:, 5 + s % 3, 0:STRIP], centre_sb[:, :], src[:, s * STRIP:(s + 1) * STRIP],
                         start=True, stop=True).then_inc(S["centred"], 1)

            def variance(b, n, s):
                e.wait_ge(S["squares"], (b * 2 + n) * NWIN + s + 1)
                for i in range(LPS):
                    k = LPS * s + i
                    mm = e.matmul(ps[0:LT, 2, k:k + 1], sq[:, s % 2, i * LT:(i + 1) * LT], mean_col[:, :],
                                  start=True, stop=True)
                mm.then_inc(S["variances"], 1)

            def turn_rstd(b, n):
                hold(e, S["rstd_low"], b * 2 + n + 1)
                e.transpose(ps[0:2 * HD, 1, 0:LT], rstd_parts[:, :], eye_sb[0:LT, 0:LT]).then_inc(S["rstd_turned"], 1)

            def spread_rstd(b, n):
                e.wait_ge(S["rstd_rows"], b * 2 + n + 1)
                for s in range(NWIN):
                    if s >= 2:
                        e.wait_ge(S["normed"], (b * 2 + n) * NWIN + s - 1)
                    for i in range(LPS):
                        k = LPS * s + i
                        mm = e.matmul(ps[:, 5 + s % 2, i * LT:(i + 1) * LT],
                                      spread_sb[:, k:k + 1].to_broadcast([2 * HD, P]), rstd_t[:, :],
                                      start=True, stop=True)
                    mm.then_inc(S["rstd_spread"], 1)

            def q_project(b, r):
                e.matmul(ps[:, 5, 0:STRIP], wqkv_sb[:, 0:P],
                         xhat[:, bass.ds(r * STRIP, STRIP)], start=True, stop=True).then_inc(S["q_made"], 1)

            def scores(b, w, half, j, queries=None):
                if queries is not None:
                    e.wait_ge(S["q_kept"], queries)
                e.wait_ge(S["k_chosen"], (b * NW + w) * TOPK + TOPK)
                slot = (half * NWIN + j) % 2
                for p in range(2):
                    mm = e.matmul(ps[:, slot, p * KEYS:(p + 1) * KEYS],
                                  q_sb[:, half, j, 2 * p:2 * p + 2, :].rearrange("p h q -> p (h q)"),
                                  ksel[:, slot, :], start=True, stop=True)
                mm.then_inc(S["scores_made"], 1)

            def lepe_place(b, t, half, k):
                if k == 0:
                    e.wait_ge(S[f"shifted{half}"], (b * SLOT_STRIPS[half] + t + 1) * ns)
                    e.wait_ge(S["lepe_kept"], b * NWIN + 2 * t + half + 1)
                ty, tx = PLACES[k]
                for g in range(HEADS):
                    src = shifted[:, half, g, :].rearrange("p (h w) -> p h w", w=VW)
                    mm = e.matmul(ps[HD * g:HD * g + HD, 6 + half, 0:STRIP], lepe_sb[:, g * NP + k, :],
                                  src[:, ty:ty + WIN, tx:tx + W], start=(k == 0), stop=(k == NP - 1))
                if k == NP - 1:
                    mm.then_inc(S["lepe_made"], 1)

            places_after = [(0, 1), (2,), (3,), (4,), (5,), (6, 7), ()]

            def image(b, first, last):
                def conv(s):
                    if not first:
                        binary_conv(b - 1, s, S["hi_done"], S["lo_done"], S["conv_kept"], S["conv_made"], False,
                                    3 + s % 2)

                e.wait_ge(S["pos_done"], b * 9 + 9)
                centre(b, 0, 0, x1)
                for s in range(5):
                    centre(b, 0, s + 1, x1)
                    conv(s)
                    variance(b, 0, s)
                centre(b, 0, 6, x1)
                variance(b, 0, 5)
                variance(b, 0, 6)
                conv(5)
                turn_rstd(b, 0)
                conv(6)
                spread_rstd(b, 0)

                e.wait_ge(S["normed"], b * 2 * NWIN + NWIN)
                if not first:
                    e.wait_ge(S["conv_kept"], b * NWIN)
                for s in range(NWIN):
                    if s >= 2:
                        e.wait_ge(S["k_kept"], b * NWIN + s - 1)
                    e.matmul(ps[:, 3 + s % 2, 0:STRIP], wqkv_sb[:, P:2 * P], xhat[:, s * STRIP:(s + 1) * STRIP],
                             start=True, stop=True).then_inc(S["k_made"], 1)
                e.wait_ge(S["win_sums"], b + 1)
                e.matmul(ps[:, 2, 0:NW], wqkv_sb[:, 0:P], win_sum[:, :], start=True, stop=True)
                e.matmul(ps[:, 2, NW:2 * NW], wqkv_sb[:, P:2 * P], win_sum[:, :], start=True,
                         stop=True).then_inc(S["win_qk_made"], 1)
                for s in range(NWIN):
                    if s >= 2:
                        e.wait_ge(S["v_kept"], b * NWIN + s - 1)
                    e.matmul(ps[:, 6 + s % 2, 0:STRIP], wqkv_sb[:, 2 * P:3 * P], xhat[:, s * STRIP:(s + 1) * STRIP],
                             start=True, stop=True).then_inc(S["v_made"], 1)
                    if s:
                        e.wait_ge(S["vt_kept"], b * 2 * NWIN + 2 * s)
                    for j in range(NWIN):
                        w = xhat[:, s * STRIP + j * WPIX:s * STRIP + (j + 1) * WPIX]
                        for o in (0, WPIX):
                            mm = e.matmul(ps[o:o + WPIX, j // 4, (j % 4) * P:(j % 4 + 1) * P], w,
                                          wqkv_sb[:, 2 * P:3 * P], start=True, stop=True)
                    mm.then_inc(S["vt_made"], 1)
                    if s == 1:
                        e.wait_ge(S["win_qk_kept"], b * 2 + 2)
                        e.matmul(ps[0:NW, 2, 128:128 + NW], qk_win[:, 0, :], qk_win[:, 1, :], start=True,
                                 stop=True).then_inc(S["logits_made"], 1)

                q_project(b, 0)
                e.wait_ge(S["v_kept"], b * NWIN + NWIN)
                e.wait_ge(S["vt_kept"], b * 2 * NWIN + 2 * NWIN)
                e.wait_ge(S["logits_kept"], b + 1)
                scores(b, 0, 0, 0, b * 4 * NWIN + 4)
                scores(b, 1, 0, 1)

                def step(t, half, j, tail):
                    r = 2 * t + half
                    n = b * NW + r * NWIN + j
                    slot = (half * NWIN + j) % 2
                    e.wait_ge(S["probs_scaled"], n * 2 + 2)
                    for p in range(2):
                        for f in range(2):
                            mm = e.transpose(ps[:, 2, (2 * p + f) * P:(2 * p + f + 1) * P],
                                             probs[:, slot, p, f * P:(f + 1) * P], eye_sb[:, :])
                    mm.then_inc(S["probs_turned"], 1)
                    if j == 2 and not tail:
                        e.wait_ge(S["q_kept"], b * 4 * NWIN + r * 4 + 4)
                        q_project(b, r + 1)
                    if j < NWIN - 2:
                        scores(b, r * NWIN + j + 2, half, j + 2)
                    elif not tail:
                        scores(b, r * NWIN + j + 2, 1 - half, j + 2 - NWIN,
                               b * 4 * NWIN + r * 4 + 8 if j == NWIN - 2 else None)
                    e.wait_ge(S["turned_kept"], n + 1)
                    e.wait_ge(S["v_chosen"], n * 4 + 4)
                    if j == 0:
                        e.wait_ge(S["mixed_kept"], b * NWIN + r + 1)
                    for f in range(2):
                        for h in range(HEADS):
                            mm = e.matmul(ps[HD * h:HD * h + HD, 3 + half, j * WPIX:(j + 1) * WPIX],
                                          vsel[:, slot, f, HD * h:HD * h + HD],
                                          probs_t[:, (2 * (h // 2) + f) * P + (h % 2) * WPIX:
                                                  (2 * (h // 2) + f) * P + (h % 2 + 1) * WPIX],
                                          start=(f == 0), stop=(f == 1))
                    mm.then_inc(S["mixed"], 1)
                    for k in places_after[j]:
                        lepe_place(b, t, half, k)
                window_rows(e, step)

                def project(s):
                    e.wait_ge(S["mixed_kept"], b * NWIN + s + 3)
                    if s >= 2:
                        e.wait_ge(S["x2_done"], b * NWIN + s - 1)
                    e.matmul(ps[:, s % 2, 0:STRIP], wo_sb[:, :], xc[:, s * STRIP:(s + 1) * STRIP], start=True,
                             stop=True).then_inc(S["projected"], 1)

                def centre2(s):
                    e.wait_ge(S["x2_done"], b * NWIN + s + 1)
                    if s == 0:
                        e.wait_ge(S["lepe_kept"], b * NWIN + NWIN + 2)
                    centre(b, 1, s, x2)
                project(0)
                project(1)
                for s in range(NWIN):
                    centre2(s)
                    if s + 2 < NWIN:
                        project(s + 2)
                    if s:
                        variance(b, 1, s - 1)
                variance(b, 1, NWIN - 1)
                turn_rstd(b, 1)
                spread_rstd(b, 1)

                def hidden(s):
                    if s == 0:
                        e.wait_ge(S["normed"], b * 2 * NWIN + 2 * NWIN)
                    for c in range(HID):
                        if s:
                            e.wait_ge(S["hidden_kept"], b * 3 * NWIN + 3 * (s - 1) + c + 1)
                        e.matmul(ps[:, 5 + c, 0:STRIP], w1_sb[:, c * P:(c + 1) * P],
                                 xhat[:, s * STRIP:(s + 1) * STRIP], start=True, stop=True).then_inc(S["hidden_made"], 1)
                hidden(0)
                for s in range(NWIN):
                    if s + 1 < NWIN:
                        hidden(s + 1)
                    e.wait_ge(S["hidden_kept"], b * 3 * NWIN + 3 * s + 3)
                    if s >= 2:
                        e.wait_ge(S["x3_done"], b * NWIN + s - 1)
                    for c in range(HID):
                        mm = e.matmul(ps[:, s % 2, 0:STRIP], w2_sb[:, c, :], hid[:, s % 2, c, :],
                                      start=(c == 0), stop=(c == HID - 1))
                    mm.then_inc(S["mlp_made"], 1)

            def binary_conv(b, s, hi_done, lo_done, kept, made, credits, bank):
                have = min(s + 2, NWIN)
                e.wait_ge(hi_done, b * NWIN + have)
                e.wait_ge(lo_done, b * NWIN + have)
                if credits:
                    e.wait_ge(kept, b * NWIN + s + 1)
                elif s >= 2:
                    e.wait_ge(kept, b * NWIN + s - 1)
                for t, (dy, dx) in enumerate(TAPS3):
                    for part in (hi, lo):
                        src = part[:, :].rearrange("p (h w) -> p h w", w=CW)
                        mm = e.matmul(ps[:, bank, 0:STRIP], cw_sign[:, t, :],
                                      src[:, WIN * s + 1 + dy:WIN * s + 1 + dy + WIN, 1 + dx:1 + dx + W],
                                      start=(t == 0 and part is hi), stop=(t == 8 and part is lo))
                mm.then_inc(made, 1)

            image_loop(e, image)
            for s in range(NWIN):
                binary_conv(nb - 1, s, S["hi_done"], S["lo_done"], S["conv_kept"], S["conv_made"], False, 3 + s % 2)

            e.sem_inc(S["b_made"], NWIN)
            e.wait_ge(S["setup_dve"], 14)
            with e.Fori(0, nb) as b:
                for s in range(NWIN):
                    binary_conv(b, s, S["b_hi"], S["b_lo"], S["b_kept"], S["b_made"], True, s)

        @block.scalar
        def _(e):
            e.sem_inc(S["b_kept"], NWIN)
            e.sem_inc(S["lepe_kept"], 2)

            def keep_centred(b, n, s):
                e.wait_ge(S["centred"], (b * 2 + n) * NWIN + s + 1)
                e.activation(xc[:, s * STRIP:(s + 1) * STRIP], ps[:, 5 + s % 3, 0:STRIP], ACT.Copy
                             ).then_inc(S["centred_copied"], 1)
                if s >= 2:
                    e.wait_ge(S["variances"], (b * 2 + n) * NWIN + s - 1)
                e.activation(sq[:, s % 2, :], ps[:, 5 + s % 3, 0:STRIP], ACT.Square).then_inc(S["squares"], 1)

            def root(b, n):
                e.wait_ge(S["eps_added"], b * 2 + n + 1)
                e.activation(ln_small[:, 1, :], ln_small[:, 0, :], ACT.Sqrt).then_inc(S["roots"], 1)

            def keep_conv(b, s):
                e.wait_ge(S["conv_made"], b * NWIN + s + 1)
                e.activation(y1[:, s * STRIP:(s + 1) * STRIP], ps[:, 3 + s % 2, 0:STRIP],
                             ACT.Copy).then_inc(S["conv_kept"], 1)

            def q_keep(b, half):
                for h in range(HEADS):
                    e.activation(q_sb[HD * h:HD * h + HD, half, :, h, :],
                                 ps[HD * h:HD * h + HD, 5, 0:STRIP].rearrange("p (j q) -> p j q", q=WPIX),
                                 ACT.Identity, bias=bq[HD * h:HD * h + HD, :], scale=SCALE).then_inc(S["q_kept"], 1)

            def exp(n, slot):
                e.wait_ge(S["max_found"], n + 1)
                for p in range(2):
                    e.activation(probs[:, slot, p, :], ps[:, slot, p * KEYS:(p + 1) * KEYS], ACT.Exp,
                                 bias=neg_max[:, slot, p:p + 1],
                                 accum_out=row_sum[:, slot, p:p + 1]).then_inc(S["exp_done"], 1)

            def image(b, first, last):
                def conv(s):
                    if not first:
                        keep_conv(b - 1, s)

                keep_centred(b, 0, 0)
                for s in range(5):
                    keep_centred(b, 0, s + 1)
                    conv(s)
                keep_centred(b, 0, 6)
                root(b, 0)
                conv(5)
                conv(6)
                for s in range(NWIN):
                    e.wait_ge(S["k_made"], b * NWIN + s + 1)
                    e.activation(k_sb[:, s * STRIP:(s + 1) * STRIP], ps[:, 3 + s % 2, 0:STRIP], ACT.Identity,
                                 bias=bk).then_inc(S["k_kept"], 1)
                for s in range(NWIN):
                    e.wait_ge(S["v_made"], b * NWIN + s + 1)
                    dst = vpad[:, :].rearrange("p (h w) -> p h w", w=VW)[:, 2 + WIN * s:2 + WIN * (s + 1), 2:2 + W]
                    e.activation(dst.rearrange("p r (x c) -> p r x c", c=WIN),
                                 ps[:, 6 + s % 2, 0:STRIP].rearrange("p (x r c) -> p r x c", r=WIN, c=WIN),
                                 ACT.Identity, bias=bv).then_inc(S["v_kept"], 1)
                e.wait_ge(S["q_made"], b * NWIN + 1)
                q_keep(b, 0)
                exp(b * NW, 0)
                exp(b * NW + 1, 1)

                def step(t, half, j, tail):
                    r = 2 * t + half
                    n = b * NW + r * NWIN + j
                    slot = (half * NWIN + j) % 2
                    e.wait_ge(S["probs_turned"], n + 1)
                    e.activation(probs_t[:, :], ps[:, 2, :], ACT.Copy).then_inc(S["turned_kept"], 1)
                    if j == 2 and not tail:
                        e.wait_ge(S["q_made"], b * NWIN + r + 2)
                        q_keep(b, 1 - half)
                    if j < NWIN - 2 or not tail:
                        exp(n + 2, slot)
                    if j == NWIN - 1:
                        e.wait_ge(S["lepe_made"], b * NWIN + r + 1)
                        e.activation(xc[:, bass.ds(r * STRIP, STRIP)], ps[:, 6 + half, 0:STRIP], ACT.Identity,
                                     bias=b_lepe).then_inc(S["lepe_kept"], 1)
                window_rows(e, step)

                for s in range(NWIN):
                    keep_centred(b, 1, s)
                root(b, 1)
                for s in range(NWIN + 1):
                    if s < NWIN:
                        if s >= 2:
                            e.wait_ge(S["mlp_made"], b * NWIN + s - 1)
                        for c in range(HID):
                            e.wait_ge(S["hidden_made"], b * 3 * NWIN + 3 * s + c + 1)
                            e.activation(hid[:, s % 2, c, :], ps[:, 5 + c, 0:STRIP], ACT.Gelu,
                                         bias=bh[c]).then_inc(S["hidden_kept"], 1)
                    if s >= 1:
                        e.wait_ge(S["x3_done"], b * NWIN + s)
                        e.activation(inner(hi, s - 1), rows(x2, s - 1), ACT.Copy).then_inc(S["hi_done"], 1)

            image_loop(e, image)
            for s in range(NWIN):
                keep_conv(nb - 1, s)

            def bn_root(k):
                e.wait_ge(S["bn_dve"], k * 10 + 2)
                e.activation(bn_sb[:, 2:3], bn_sb[:, 1:2], ACT.Sqrt).then_inc(S["bn_act"], 1)

            bn_root(0)
            e.wait_ge(S["bn_dve"], 6)

            def part_b(t, i):
                b = t * 2 + i
                yin, yout = arena[:, i * PIX:(i + 1) * PIX], arena[:, (2 + i) * PIX:(3 + i) * PIX]
                e.wait_ge(S[f"b_loaded{i}"], 16 * t + 16)
                e.wait_ge(S[f"b_stored{i}"], 16 * t + 16)
                e.wait_ge(S["b_stats"], t * 2 * NWIN + 2 * NWIN)
                for s in range(NWIN + 2):
                    if s < NWIN:
                        e.wait_ge(S["b_made"], b * NWIN + min(s + 2, NWIN))
                        ys = yin[:, s * STRIP:(s + 1) * STRIP]
                        e.activation(ys, ys, ACT.Relu, bias=bn_sb[:, 5:6], scale=bn_sb[:, 4:5]).then_inc(S["relu_done"], 1)
                        e.wait_ge(S["relu_done"], b * NWIN + s + 1)
                        e.activation(inner(hi, s), rows(yin, s), ACT.Copy).then_inc(S["b_hi"], 1)
                    if s >= 2:
                        e.wait_ge(S["b_made"], b * NWIN + NWIN + s - 1)
                        e.activation(yout[:, (s - 2) * STRIP:(s - 1) * STRIP], ps[:, s - 2, 0:STRIP],
                                     ACT.Copy).then_inc(S["b_kept"], 1)
            with e.Fori(0, nb // 2) as t:
                part_b(t, 0)
                part_b(t, 1)
            bn_root(1)
            e.wait_ge(S["bn_dve"], 16)
            with e.Fori(0, nb // 2) as t:
                for i in range(2):
                    e.wait_ge(S["c_sum"], t * 2 + i + 1)
                    u = arena[:, 2 * i * PIX:(2 * i + 1) * PIX]
                    e.activation(u, u, ACT.Relu, bias=bn_sb[:, 5:6]).then_inc(S["c_relu"], 1)

        @block.gpsimd
        def _(e):
            e.memset(q_sb[:, :, :, :, :], 0.0).then_inc(S["pad_zero"], 1)
            e.memset(vpad[:, :], 0.0).then_inc(S["pad_zero"], 1)
            e.memset(hi[:, :].bitcast(F32), 0.0).then_inc(S["pad_zero"], 1)
            e.memset(lo[:, :].bitcast(F32), 0.0).then_inc(S["pad_zero"], 1)
            e.memset(mean_col[:, :], 1.0 / P).then_inc(S["pad_zero"], 1)
            e.memset(rstd_parts[:, :], 0.0).then_inc(S["pad_zero"], 1)
            regs = [e.alloc_register(f"pool_key{i}") for i in range(TOPK)]

            def choose(b, r, slot, j):
                w = r * NWIN + j
                n = b * NW + w
                e.load(regs, key_off[0:1, bass.ds(w * TOPK, TOPK)])
                at = [e.snap(q, min_val=0, max_val=(NW - 1) * WPIX) for q in regs]
                hold(e, S["mixed"], n + 1)
                for i in range(TOPK):
                    o = WPIX * (i % 2)
                    e.tensor_copy(vsel[o:o + WPIX, slot, i // 2, :],
                                  vt[o:o + WPIX, bass.ds(at[i] * 2, P)]).then_inc(S["v_chosen"], 1)

            def image(b, first, last):
                e.wait_ge(S["offsets_placed"], b * 16 + 16)
                hold(e, S["vt_kept"], b * 2 * NWIN + 2 * NWIN)
                window_rows(e, lambda t, half, j, tail: choose(b, 2 * t + half, (half * NWIN + j) % 2, j))
            e.sem_inc(S["mixed"], 2)
            image_loop(e, image)

        @block.vector
        def _(e):
            e.wait_ge(S["setup_loaded"], 144)
            e.wait_ge(S["setup_pe"], 1)
            e.wait_ge(S["pad_zero"], 6)
            n_setup = [0]

            def mark(ins):
                n_setup[0] += 1
                ins.then_inc(S["setup_dve"], 1)

            mark(e.tensor_tensor(bias[:, 0:3], ps[:, 0, 0:3], vec_sb[:, VEC["qkv_b"]:VEC["qkv_b"] + 3], ALU.add))
            mark(e.tensor_tensor(bias[:, 3:6], ps[:, 0, 3:6], vec_sb[:, VEC["mlp_b1"]:VEC["mlp_b1"] + 3], ALU.add))
            mark(e.tensor_scalar(wqkv_sb[:, :], wqkv_sb[:, :], v_("ln1_g"), None, ALU.mult))
            mark(e.tensor_scalar(w1_sb[:, :], w1_sb[:, :], v_("ln2_g"), None, ALU.mult))
            for o in (0, HD):
                mark(e.tensor_copy(spread_sb[o:o + HD, :], eye_sb[o:o + HD, o:o + NLT]))
            mark(e.tensor_scalar(pos_centre, v_("pos_w", 4), 1.0, None, ALU.add))
            mark(e.tensor_tensor(lepe_sb[:, :, :], eye4_sb[:, :].unsqueeze(1).to_broadcast([P, HEADS * NP, HD]),
                                 vec_sb[:, VEC["lepe_taps"]:VEC["lepe_taps"] + HEADS * NP].unsqueeze(2)
                                 .to_broadcast([P, HEADS * NP, HD]), ALU.mult))
            def signs():
                negative, raw = k_sb[:, 0:9 * P], xhat[:, 0:9 * P]
                mark(e.tensor_scalar(negative, raw, 0.0, None, ALU.is_lt))
                e.wait_ge(S["setup_dve"], n_setup[0])
                mark(e.scalar_tensor_tensor(out=cw_sign[:, :, :].rearrange("p t c -> p (t c)"), in0=raw,
                                            scalar=0.0, in1=negative, op0=ALU.is_gt, op1=ALU.subtract))
            signs()
            e.wait_ge(S["setup_dve"], n_setup[0])
            mark(e.tensor_tensor(b_lepe, v_("lepe_b"), bv, ALU.add))
            mark(e.tensor_scalar(bq, bq, SCALE, None, ALU.mult))
            e.wait_ge(S["setup_dve"], n_setup[0])
            e.sem_inc(S["mixed_kept"], 2)
            e.sem_inc(S["b_stats"], 2 * NWIN)

            order = [4, 0, 1, 2, 3, 5, 6, 7, 8]

            def pos_tap(base, k):
                t = order[k]
                dy, dx = TAPS3[t]
                if k == 0:
                    e.tensor_scalar(x1, xin, pos_centre, v_("pos_b"), ALU.mult, ALU.add).then_inc(S["pos_done"], 1)
                    return
                a, i = (z.rearrange("p (h w) -> p h w", w=W) for z in (x1, xin))
                y0, y1 = max(0, -dy), H - max(0, dy)
                c0, c1 = max(0, -dx), W - max(0, dx)
                e.wait_ge(S["pos_done"], base + k)
                acc = a[:, y0:y1, c0:c1]
                e.scalar_tensor_tensor(out=acc, in0=i[:, y0 + dy:y1 + dy, c0 + dx:c1 + dx], scalar=v_("pos_w", t),
                                       in1=acc, op0=ALU.mult, op1=ALU.add).then_inc(S["pos_done"], 1)

            def rstd(b, n):
                k = b * 2 + n + 1
                e.wait_ge(S["variances"], k * NWIN)
                e.tensor_scalar(ln_small[:, 0, :], ps[0:LT, 2, 0:NLT], LN_EPS, None, ALU.add).then_inc(S["eps_added"], 1)
                e.wait_ge(S["roots"], k)
                e.reciprocal(ln_small[:, 0, :], ln_small[:, 1, :]).then_inc(S["rstd"], 1)
                e.wait_ge(S["rstd"], k)
                e.tensor_copy(rstd_parts[:, 0:NLT].bitcast(F32R), ln_small[:, 0, :]).then_inc(S["rstd_high"], 1)
                e.wait_ge(S["rstd_high"], k)
                e.tensor_tensor(rstd_parts[:, HD:HD + NLT].bitcast(F32R), ln_small[:, 0, :], rstd_parts[:, 0:NLT],
                                ALU.subtract).then_inc(S["rstd_low"], 1)
                e.wait_ge(S["rstd_turned"], k)
                e.tensor_copy(rstd_t[:, :], ps[0:2 * HD, 1, 0:LT]).then_inc(S["rstd_rows"], 1)

            def normalise(b, n, put):
                e.wait_ge(S["centred_copied"], (b * 2 + n + 1) * NWIN)
                for s in range(NWIN):
                    e.wait_ge(S["rstd_spread"], (b * 2 + n) * NWIN + s + 1)
                    e.tensor_tensor(put(xhat, s), img(xc, s),
                                    ps[:, 5 + s % 2, 0:STRIP].rearrange("p (r x c) -> p r x c", r=WIN, c=WIN),
                                    ALU.mult).then_inc(S["normed"], 1)

            regs = [e.alloc_register(f"dve_key{i}") for i in range(TOPK)]

            def choose(b, w, slot):
                e.load(regs, key_off[0:1, bass.ds(w * TOPK, TOPK)])
                at = [e.snap(q, min_val=0, max_val=(NW - 1) * WPIX) for q in regs]
                for i in range(TOPK):
                    e.tensor_copy(ksel[:, slot, i * WPIX:(i + 1) * WPIX],
                                  k_sb[:, bass.ds(at[i], WPIX)]).then_inc(S["k_chosen"], 1)

            def row_max(n, slot):
                e.wait_ge(S["scores_made"], n + 1)
                e.tensor_reduce(neg_max[:, slot, :], ps[:, slot, :].rearrange("p (a k) -> p a k", a=2), AX.X,
                                ALU.max, negate=True).then_inc(S["max_found"], 1)

            def invert_sums(n, slot):
                e.wait_ge(S["exp_done"], n * 2 + 2)
                e.reciprocal(row_inv[:, slot, :], row_sum[:, slot, :]).then_inc(S["inv_done"], 1)

            def scale_probs(n, slot):
                e.wait_ge(S["inv_done"], n + 1)
                for p in range(2):
                    e.tensor_scalar(probs[:, slot, p, :], probs[:, slot, p, :], row_inv[:, slot, p:p + 1], None,
                                    ALU.mult).then_inc(S["probs_scaled"], 1)

            def conv_stats(b, s):
                e.wait_ge(S["conv_kept"], b * NWIN + s + 1)
                e.bn_stats(stats[:, bass.ds(b * NWIN + s, 1), :].rearrange("p a k -> p (a k)"),
                           y1[:, s * STRIP:(s + 1) * STRIP]).then_inc(S["conv_stats"], 1)

            for k in range(9):
                if k == 0:
                    e.wait_ge(S["x_loaded"], 16)
                pos_tap(0, k)

            def image(b, first, last):
                if not first:
                    for s in range(5):
                        conv_stats(b - 1, s)
                rstd(b, 0)
                normalise(b, 0, win)
                e.wait_ge(S["normed"], b * 2 * NWIN + NWIN)
                e.tensor_reduce(win_sum[:, :], xhat.rearrange("p (w q) -> p w q", q=WPIX), AX.X,
                                ALU.add).then_inc(S["win_sums"], 1)
                if not first:
                    conv_stats(b - 1, 5)
                    conv_stats(b - 1, 6)
                e.wait_ge(S["win_qk_made"], b + 1)
                e.tensor_scalar(qk_win[:, 0, :], ps[:, 2, 0:NW], SCALE / WPIX, bq, ALU.mult,
                                ALU.add).then_inc(S["win_qk_kept"], 1)
                e.tensor_scalar(qk_win[:, 1, :], ps[:, 2, NW:2 * NW], 1.0 / WPIX, bk, ALU.mult,
                                ALU.add).then_inc(S["win_qk_kept"], 1)
                if not first:
                    e.wait_ge(S["y1_stored"], b * 16)
                for s in range(NWIN):
                    e.wait_ge(S["vt_made"], b * NWIN + s + 1)
                    e.tensor_copy(vt[:, s * NWIN * P:(s * NWIN + 4) * P], ps[:, 0, :]).then_inc(S["vt_kept"], 1)
                    e.tensor_copy(vt[:, (s * NWIN + 4) * P:(s + 1) * NWIN * P], ps[:, 1, 0:3 * P]
                                  ).then_inc(S["vt_kept"], 1)
                    if s == 1:
                        e.wait_ge(S["logits_made"], b + 1)
                        e.tensor_copy(logits[:, :], ps[0:NW, 2, 128:128 + NW]).then_inc(S["logits_kept"], 1)
                        hold(e, S["logits_kept"], b + 1)
                        e.max(top8[:, :], logits[:, :]).then_inc(S["top_values"], 1)
                    if s == 2:
                        hold(e, S["top_values"], b + 1)
                        e.max_index(top_i[:, :], top8[:, :], logits[:, :]).then_inc(S["top_found"], 1)
                        e.wait_ge(S["top_found"], b + 1)
                        e.tensor_scalar(top_off[:, :], top_i[:, 0:TOPK], float(WPIX), None, ALU.mult
                                        ).then_inc(S["offsets"], 1)

                e.wait_ge(S["k_kept"], b * NWIN + NWIN)
                hold(e, S["offsets_placed"], b * 16 + 16)
                choose(b, 0, 0)
                choose(b, 1, 1)
                row_max(b * NW, 0)
                choose(b, 2, 0)
                row_max(b * NW + 1, 1)
                invert_sums(b * NW, 0)
                scale_probs(b * NW, 0)

                def step(t, half, j, tail):
                    r = 2 * t + half
                    w = r * NWIN + j
                    n = b * NW + w
                    slot = (half * NWIN + j) % 2
                    if j < NWIN - 1 or not tail:
                        invert_sums(n + 1, 1 - slot)
                    if j < NWIN - 3 or not tail:
                        choose(b, w + 3, 1 - slot)
                    if j < NWIN - 1 or not tail:
                        scale_probs(n + 1, 1 - slot)
                    if j < NWIN - 2 or not tail:
                        row_max(n + 2, slot)
                    if j == NWIN - 1:
                        e.wait_ge(S["mixed"], n + 3)
                        e.wait_ge(S["lepe_kept"], b * NWIN + r + 3)
                        dst = xc[:, bass.ds(r * STRIP, STRIP)].rearrange("p (r x c) -> p r x c", r=WIN, c=WIN)
                        e.tensor_tensor(dst, dst, ps[:, 3 + half, 0:STRIP].rearrange("p (x r c) -> p r x c", r=WIN,
                                                                                   c=WIN),
                                        ALU.add).then_inc(S["mixed_kept"], 1)
                window_rows(e, step)

                e.wait_ge(S["x3_stored"], b * 16 + 16)
                for s in range(NWIN):
                    e.wait_ge(S["projected"], b * NWIN + s + 1)
                    e.scalar_tensor_tensor(out=x2[:, s * STRIP:(s + 1) * STRIP], in0=ps[:, s % 2, 0:STRIP],
                                           scalar=v_("wo_b"), in1=x1[:, s * STRIP:(s + 1) * STRIP], op0=ALU.add,
                                           op1=ALU.add).then_inc(S["x2_done"], 1)
                rstd(b, 1)
                normalise(b, 1, img)
                for s in range(NWIN):
                    e.wait_ge(S["mlp_made"], b * NWIN + s + 1)
                    xs = x2[:, s * STRIP:(s + 1) * STRIP]
                    e.scalar_tensor_tensor(out=xs, in0=ps[:, s % 2, 0:STRIP], scalar=v_("mlp_b2"), in1=xs,
                                           op0=ALU.add, op1=ALU.add).then_inc(S["x3_done"], 1)
                    if not last:
                        if s == 0:
                            e.wait_ge(S["x_loaded"], b * 16 + 32)
                        for k in range(9 * s // NWIN, 9 * (s + 1) // NWIN):
                            pos_tap(b * 9 + 9, k)
                    e.wait_ge(S["hi_done"], b * NWIN + s + 1)
                    e.tensor_tensor(inner(lo, s), rows(x2, s), inner(hi, s).bitcast(F32),
                                    ALU.subtract).then_inc(S["lo_done"], 1)

            image_loop(e, image)
            for s in range(NWIN):
                conv_stats(nb - 1, s)

            def batch_norm(k, counted, credits, gamma, beta):
                def m(ins, n):
                    ins.then_inc(S["bn_dve"], n)
                e.wait_ge(counted, nb * NWIN + credits)
                m(e.bn_aggr(bn_sb[:, 0:2], stats[:, :, :].rearrange("p a k -> p (a k)")), 1)
                e.wait_ge(S["bn_dve"], k * 10 + 1)
                m(e.tensor_scalar(bn_sb[:, 1:2], bn_sb[:, 1:2], BN_EPS, None, ALU.add), 1)
                e.wait_ge(S["bn_act"], k + 1)
                m(e.reciprocal(bn_sb[:, 3:4], bn_sb[:, 2:3]), 1)
                e.wait_ge(S["bn_dve"], k * 10 + 3)
                if k:
                    e.wait_ge(S["relu_done"], nb * NWIN)
                m(e.tensor_tensor(bn_sb[:, 4:5], bn_sb[:, 3:4], gamma, ALU.mult), 1)
                e.wait_ge(S["bn_dve"], k * 10 + 4)
                m(e.tensor_tensor(bn_sb[:, 2:3], bn_sb[:, 0:1], bn_sb[:, 4:5], ALU.mult), 1)
                e.wait_ge(S["bn_dve"], k * 10 + 5)
                m(e.tensor_tensor(bn_sb[:, 5:6], beta, bn_sb[:, 2:3], ALU.subtract), 5)

            batch_norm(0, S["conv_stats"], 0, v_("gamma1"), v_("beta1"))
            e.wait_ge(S["signs2_loaded"], 16)
            signs()

            def part_b(t, i):
                b = t * 2 + i
                yin = arena[:, i * PIX:(i + 1) * PIX]
                for s in range(NWIN + 2):
                    if s < NWIN:
                        e.wait_ge(S["b_hi"], b * NWIN + s + 1)
                        e.tensor_tensor(inner(lo, s), rows(yin, s), inner(hi, s).bitcast(F32),
                                        ALU.subtract).then_inc(S["b_lo"], 1)
                    if s >= 2:
                        e.wait_ge(S["b_kept"], b * NWIN + NWIN + s - 1)
                        e.bn_stats(stats[:, bass.ds(b * NWIN + s - 2, 1), :].rearrange("p a k -> p (a k)"),
                                   arena[:, (2 + i) * PIX + (s - 2) * STRIP:(2 + i) * PIX + (s - 1) * STRIP]).then_inc(S["b_stats"], 1)
            e.wait_ge(S["bn_dve"], 10)
            with e.Fori(0, nb // 2) as t:
                part_b(t, 0)
                part_b(t, 1)
            batch_norm(1, S["b_stats"], 2 * NWIN, v_("gamma2"), v_("beta2"))
            e.wait_ge(S["bn_dve"], 20)
            with e.Fori(0, nb // 2) as t:
                for i in range(2):
                    e.wait_ge(S[f"c_loaded{i}"], 32 * t + 32)
                    u = arena[:, 2 * i * PIX:(2 * i + 1) * PIX]
                    e.scalar_tensor_tensor(out=u, in0=u, scalar=bn_sb[:, 4:5],
                                           in1=arena[:, (2 * i + 1) * PIX:(2 * i + 2) * PIX], op0=ALU.mult,
                                           op1=ALU.add).then_inc(S["c_sum"], 1)


def lay_out(inputs, nb):
    f = {k: np.asarray(v) for k, v in inputs.items()}
    vec = np.zeros((P, NVEC), np.float32)

    def put(name, a, k=1):
        vec[:, VEC[name]:VEC[name] + k] = a

    L0 = "L0_conv_"
    put("pos_w", f[L0 + "pos_w"].reshape(P, 9), 9)
    for name in ("pos_b", "ln1_g", "ln1_b", "lepe_b", "wo_b", "ln2_g", "ln2_b", "mlp_b2"):
        put(name, f[L0 + name].reshape(P, 1))
    put("qkv_b", f[L0 + "qkv_b"].reshape(3, P).T, 3)
    put("mlp_b1", f[L0 + "mlp_b1"].reshape(HID, P).T, HID)
    for name in ("gamma1", "beta1", "gamma2", "beta2"):
        put(name, f["L1_conv_" + name].reshape(P, 1))
    lepe = f[L0 + "lepe_w"].reshape(P, 5, 5)
    for t, row in enumerate(lepe_cover()):
        for k, tap in enumerate(row):
            for g in range(HEADS):
                if tap is not None:
                    vec[HD * k:HD * k + HD, VEC["lepe_taps"] + g * NP + t] = lepe[HD * g:HD * g + HD, tap[0], tap[1]]

    def conv(w):
        return np.ascontiguousarray(w.transpose(1, 2, 3, 0).reshape(P, 9 * P))

    eye = np.eye(P, dtype=np.float32)
    return {
        "x": np.ascontiguousarray(f["x"].reshape(-1, P, PIX)[:nb]),
        "vec": vec,
        "wqkv": f[L0 + "qkv_w"], "wo": f[L0 + "wo_w"], "w1": f[L0 + "mlp_w1"], "w2": f[L0 + "mlp_w2"],
        "cw1": conv(f["L1_conv_w1"]), "cw2": conv(f["L1_conv_w2"]),
        "eye": eye, "centre": eye - np.float32(1.0 / P), "eye4": np.tile(eye[0:HD, 0:HD], (4, 1)),
    }


def kernel(**inputs):
    import concourse.bacc as _bacc
    from concourse.bass_utils import run_bass_kernel_spmd as _run

    nb = inputs["x"].shape[0]
    arrays = lay_out(inputs, nb)
    nc = _bacc.Bacc("TRN2", target_bir_lowering=False, num_devices=1)
    aps = {n: nc.dram_tensor(n, a.shape, F32, kind="ExternalInput").ap() for n, a in arrays.items()}
    out = nc.dram_tensor("out", (nb, P, PIX), F32, kind="ExternalOutput").ap()
    build(nc, **aps, out=out, nb=nb)
    r = _run(nc, [arrays], core_ids=[0])
    return r.results[0]["out"].reshape(nb, P, H, W)
```

```python
from contextlib import ExitStack

import numpy as np

import concourse.bass as bass
from concourse import mybir

F32 = mybir.dt.float32
F32R = mybir.dt.float32r
U32 = mybir.dt.uint32
ALU = mybir.AluOpType
ACT = mybir.ActivationFunctionType
AX = mybir.AxisListType

P = 128
H = W = 56
PIX = H * W
NWIN = 7
WIN = 8
WPIX = WIN * WIN
NW = NWIN * NWIN
STRIP = WIN * W
HEADS, HD = 4, 32
TOPK = 4
KEYS = TOPK * WPIX
PAIR = 2 * WPIX
HID = 3
SCALE = float(P) ** -0.5
LN_EPS = 1e-6
BN_EPS = 1e-5
LT = 112
NLT = PIX // LT
LPS = STRIP // LT
Y2_SLOTS = 10
Y1_HEAD = 5

SHIFTS = [(0, sx) for sx in range(4)]
PLACES = [(ty, 0) for ty in range(5)]
RIGHT_TAPS = [(ty, 4) for ty in range(5)]
NS, NP = len(SHIFTS), len(PLACES)
VW = W + 4
VROWS = H + 5
RLEN = (WIN + 4) * VW
CW = W + 2
TAPS3 = [(dy, dx) for dy in (-1, 0, 1) for dx in (-1, 0, 1)]

VEC = {}
_n = 0
for _name, _k in [("pos_w", 9), ("pos_b", 1), ("ln1_g", 1), ("ln1_b", 1), ("qkv_b", 3), ("lepe_b", 1),
                  ("wo_b", 1), ("ln2_g", 1), ("ln2_b", 1), ("mlp_b1", HID), ("mlp_b2", 1), ("gamma1", 1),
                  ("beta1", 1), ("gamma2", 1), ("beta2", 1), ("lepe_taps", HEADS * NP),
                  ("lepe_right", 5)]:
    VEC[_name] = _n
    _n += _k
NVEC = _n


def build(nc, x, vec, wqkv, wo, w1, w2, cw1, cw2, eye, centre, eye4, out, nb, dump=None):
    x3_dram = nc.dram_tensor("x3_scratch", [nb, P, PIX], F32).ap()
    y1_dram = nc.dram_tensor("y1_scratch", [nb, P, PIX], F32).ap()
    y2_dram = nc.dram_tensor("y2_scratch", [nb, P, PIX], F32).ap()

    with ExitStack() as ctx:
        def sb(name, shape, dt=F32):
            return ctx.enter_context(nc.sbuf_tensor(name, shape, dt))

        def sem(name):
            return ctx.enter_context(nc.semaphore(name))

        ps = ctx.enter_context(nc.psum_tensor("ps", [P, 8, 512], F32))

        vec_sb = sb("vec_sb", [P, NVEC])
        eye_sb = sb("eye_sb", [P, P])
        centre_sb = sb("centre_sb", [P, P])
        eye4_sb = sb("eye4_sb", [P, HD])
        mean_col = sb("mean_col", [P, 1])
        spread_sb = sb("spread_sb", [2 * HD, NLT], F32R)
        wqkv_sb = sb("wqkv_sb", [P, 3 * P])
        wo_sb = sb("wo_sb", [P, P])
        w1_high = sb("w1_high", [P, HID * P], F32R)
        w1_low = sb("w1_low", [P, HID * P], F32R)
        w2_sb = sb("w2_sb", [P, HID, P])
        cw_sign = sb("cw_sign", [P, 9, P], F32R)
        lepe_sb = sb("lepe_sb", [P, HEADS * NP, HD])
        bias = sb("bias", [P, 10])
        bq, bk, bv = (bias[:, i:i + 1] for i in range(3))
        bh = [bias[:, 3 + c:4 + c] for c in range(HID)]
        b_lepe = bias[:, 6:7]
        pos_centre = bias[:, 7:8]

        def v_(name, i=0):
            return vec_sb[:, VEC[name] + i:VEC[name] + i + 1]

        QLEN, VPLEN, SHLEN = 2 * NWIN * HEADS * WPIX, VROWS * VW, 2 * HEADS * RLEN
        at_q = 6 * PIX
        at_vpad = at_q + QLEN
        at_shifted = at_vpad + VPLEN
        at_vt = at_shifted + SHLEN
        arena = sb("arena", [P, at_vt + NW * P])
        assert at_vt + NW * P >= (2 + Y2_SLOTS) * PIX
        xin = arena[:, 0:PIX]
        streams = [arena[:, PIX:2 * PIX], arena[:, 2 * PIX:3 * PIX]]
        xc = arena[:, 3 * PIX:4 * PIX]
        xhat = arena[:, 4 * PIX:5 * PIX]
        k_sb = arena[:, 5 * PIX:6 * PIX]
        w1_sb = k_sb[:, 9 * P:(9 + HID) * P]
        q_sb = arena[:, at_q:at_vpad].rearrange("p (a j h q) -> p a j h q", a=2, j=NWIN, h=HEADS)
        vpad = arena[:, at_vpad:at_shifted]
        shifted = arena[:, at_shifted:at_vt].rearrange("p (a g n) -> p a g n", a=2, g=HEADS)
        hid = shifted[:, :, 0:2, :].rearrange("p a g n -> p a (g n)")[:, :, 0:HID * STRIP].rearrange(
            "p a (c n) -> p a c n", c=HID)
        sq = hid[:, :, 0, :]
        vt = arena[:, at_vt:at_vt + NW * P]
        def y1(s):
            return (vt if s < Y1_HEAD else k_sb)[:, s * STRIP:(s + 1) * STRIP]
        vsel = sb("vsel", [P, 2, 2, P])
        ksel = sb("ksel", [P, 2, KEYS])
        probs = sb("probs", [P, 2, 2, KEYS])
        probs_t = sb("probs_t", [P, 4 * P])
        neg_max = sb("neg_max", [P, 2, 2])
        row_sum = sb("row_sum", [P, 2, 2])
        row_inv = sb("row_inv", [P, 2, 2])
        ln_small = sb("ln_small", [LT, 2, NLT])
        rstd_parts = sb("rstd_parts", [LT, 2 * HD])
        rstd_t = sb("rstd_t", [2 * HD, LT], F32R)
        win_sum = sb("win_sum", [P, NW])
        qk_win = sb("qk_win", [P, 2, NW])
        logits = sb("logits", [NW, NW])
        top8 = sb("top8", [NW, 8])
        top_i = sb("top_i", [NW, 8], U32)
        top_off = sb("top_off", [NW, TOPK], U32)
        key_off = sb("key_off", [1, NW * TOPK], U32)
        hi = sb("hi", [P, CW * CW], F32R)
        lo = sb("lo", [P, CW * CW], F32R)
        stats = sb("stats", [P, nb * NWIN, 6])
        bn_sb = sb("bn_sb", [P, 6])

        def vt_windows(s):
            return vt[:, s * NWIN * P:(s + 1) * NWIN * P].rearrange("p (w c) -> p w c", c=P)

        def img(t, s):
            return t[:, s * STRIP:(s + 1) * STRIP].rearrange("p (r x c) -> p r x c", r=WIN, c=WIN)

        def win(t, s):
            return t[:, s * STRIP:(s + 1) * STRIP].rearrange("p (x r c) -> p r x c", r=WIN, c=WIN)

        def inner(t, s):
            return t[:, :].rearrange("p (h w) -> p h w", w=CW)[:, 1 + WIN * s:1 + WIN * (s + 1), 1:1 + W]

        def xhat_high(s):
            return inner(hi, s)

        def xhat_low(s):
            return inner(lo, s)

        def rows(t, s):
            return t[:, s * STRIP:(s + 1) * STRIP].rearrange("p (r w) -> p r w", w=W)

        S = {n: sem(n) for n in (
            "vec_loaded", "setup_loaded", "setup_dve", "setup_pe", "x_loaded", "pos_done",
            "centred", "centred_copied", "squares", "variances", "eps_added", "roots", "rstd", "rstd_high",
            "rstd_low", "rstd_turned", "k_chosen",
            "xhat_high_done", "xhat_low_done",
            "rstd_rows", "rstd_spread", "normed",
            "k_made", "v_made", "vt_made", "k_kept", "v_kept", "vt_kept", "vt_crossed",
            "win_sums", "win_qk_made", "win_qk_kept", "logits_made", "logits_kept", "top_values", "top_found",
            "offsets", "offsets_placed",
            "q_made", "q_kept", "scores_made", "max_found", "exp_done", "inv_done", "probs_scaled",
            "probs_turned", "turned_kept", "v_chosen", "mixed", "mixed_kept",
            "shifted0", "shifted1", "lepe_made", "lepe_kept", "lepe_tapped", "projected", "x2_done",
            "hidden_made", "hidden_kept", "mlp_made", "x3_done", "hi_done", "lo_done",
            "conv_made", "conv_kept", "conv_stats", "x3_stored", "y1_head_stored", "y1_tail_stored",
            "b_loaded0", "b_loaded1", "relu_done", "b_hi", "b_lo", "b_made", "b_kept", "b_stats", "y2_stored",
             "bn_dve", "bn_act", "c_loaded0", "c_loaded1", "c_sum", "c_relu", "c_stored0",
            "c_stored1", "pad_zero", "signs2_loaded", "held")}

        ns = len(SHIFTS) * HEADS * 16
        VT_BANKS = (0, 1, 3, 4)
        B_LAG = 4
        SPREAD_BANK = (5, 0)
        SLOT_STRIPS = (4, 3)

        def slot_(slot, start=0, length=PIX):
            return arena[:, bass.ds(slot * PIX + start, length)]

        wrap = min(nb, Y2_SLOTS)
        streamed = nb - wrap
        kept_here = nb - streamed
        assert nb % 2 == 0 and streamed <= Y2_SLOTS - 4

        block = ctx.enter_context(nc.Block())

        def hold(e, which, value):
            e.wait_ge(which, value)
            e.sem_inc(S["held"], 1)

        def image_loop(e, body):
            assert nb % 2 == 0
            body(0, 0, 0, True, False)
            if nb > 2:
                with e.Fori(0, nb // 2 - 1) as t:
                    body(2 * t + 1, t, 1, False, False)
                    body(2 * t + 2, t + 1, 0, False, False)
            body(nb - 1, nb // 2 - 1, 1, False, True)

        def image_loop_b(e, body):
            body(0, 0, 0, 2, None, None)
            with e.Fori(0, wrap // 2 - 1) as t:
                body(2 * t + 1, t, 1, 2 * t + 3, 2 * t + 2, None)
                body(2 * t + 2, t + 1, 0, 2 * t + 4, 2 * t + 3, None)
            body(wrap - 1, wrap // 2 - 1, 1, wrap + 1, wrap, None)
            if streamed:
                body(wrap, wrap // 2, 0, 2, wrap + 1, 0)
                with e.Fori(0, streamed // 2 - 1) as t:
                    body(2 * t + wrap + 1, t + wrap // 2, 1, 2 * t + 3, 2 * t + 2, 2 * t + 1)
                    body(2 * t + wrap + 2, t + wrap // 2 + 1, 0, 2 * t + 4, 2 * t + 3, 2 * t + 2)
                body(nb - 1, nb // 2 - 1, 1, streamed + 1, streamed, streamed - 1)

        def kept_loop(e, body):
            first = wrap - streamed
            def pairs(n, k, slot):
                if n > 0:
                    with e.Fori(0, n) as t:
                        for i in range(2):
                            body(2 * t + k + i, 2 * t + slot + i, i, False)
            pairs(first // 2 - (0 if streamed else 1), 0, 2 + streamed)
            pairs(streamed // 2 - 1, first, 2)
            for i in range(2):
                body(kept_here - 2 + i, (streamed if streamed else wrap) + i, i, True)

        def window_rows(e, step):
            def row(t, half, head=False, tail=False):
                for j in range(NWIN):
                    step(t, half, j, head, tail)
            row(0, 0, head=True)
            with e.Fori(0, (NWIN - 3) // 2) as t:
                row(t, 1)
                row(t + 1, 0)
            row((NWIN - 3) // 2, 1)
            row(NWIN // 2, 0, tail=True)

        @block.sync
        def _(e):
            e.dma_start(vec_sb[:, :], vec).then_inc(S["vec_loaded"], 16)
            e.dma_start(xin, x[0]).then_inc(S["x_loaded"], 16)
            loads = [(eye_sb, eye), (centre_sb, centre), (eye4_sb, eye4), (wqkv_sb, wqkv),
                     (wo_sb, wo), (w1_sb, w1)]
            for dst, src in loads:
                e.dma_start(dst[:, :], src).then_inc(S["setup_loaded"], 16)
            e.dma_start(w2_sb[:, :, :], w2.rearrange("(c p) n -> p c n", p=P)).then_inc(S["setup_loaded"], 16)
            e.dma_start(xhat[:, 0:9 * P], cw1).then_inc(S["setup_loaded"], 16)

            head, tail = slice(0, Y1_HEAD * STRIP), slice(Y1_HEAD * STRIP, PIX)

            def store_y1_head(b):
                hold(e, S["conv_kept"], b * NWIN + Y1_HEAD)
                e.dma_start(y1_dram[bass.ds(b, 1)].rearrange("a p n -> (a p) n")[:, head],
                            vt[:, head]).then_inc(S["y1_head_stored"], 16)

            def store_y1_tail(b):
                hold(e, S["conv_kept"], b * NWIN + NWIN)
                e.dma_start(y1_dram[bass.ds(b, 1)].rearrange("a p n -> (a p) n")[:, tail],
                            k_sb[:, tail]).then_inc(S["y1_tail_stored"], 16)

            def image(b, pair, odd, first, last):
                if not last:
                    hold(e, S["pos_done"], b * 9 + 9)
                    e.dma_start(xin, x[bass.ds(b + 1, 1)].rearrange("a p n -> (a p) n")).then_inc(S["x_loaded"], 16)
                if not first:
                    store_y1_head(b - 1)
                for s in range(NWIN):
                    if s < NWIN - 1:
                        hold(e, S["v_kept"], b * NWIN + s + 2)
                    if s >= 2:
                        e.wait_ge(S["lepe_made"], b * NWIN + s - 1)
                    for k, (sy, sx) in enumerate(SHIFTS):
                        for g in range(HEADS):
                            at = WIN * s * VW + sy * VW + sx
                            e.dma_start(shifted[HD * k:HD * k + HD, s % 2, g, :],
                                        vpad[HD * g:HD * g + HD, at:at + RLEN]).then_inc(S[f"shifted{s % 2}"], 16)
                if not first:
                    store_y1_tail(b - 1)
                for at, done in ((slice(0, 4 * STRIP), 4), (slice(4 * STRIP, PIX), NWIN)):
                    hold(e, S["x3_done"], b * NWIN + done)
                    e.dma_start(x3_dram[bass.ds(b, 1)].rearrange("a p n -> (a p) n")[:, at],
                                streams[odd][:, at]).then_inc(S["x3_stored"], 16)

            e.sem_inc(S["x3_stored"], 32)
            e.sem_inc(S["y1_tail_stored"], 16)
            image_loop(e, image)
            e.wait_ge(S["y1_head_stored"], 32)
            e.wait_ge(S["y1_tail_stored"], 48)
            e.wait_ge(S["pos_done"], 9 * nb)
            e.wait_ge(S["x3_stored"], 32 * nb)
            for i in range(2):
                e.dma_start(slot_(i), y1_dram[i]).then_inc(S[f"b_loaded{i}"], 16)
            store_y1_head(nb - 1)
            store_y1_tail(nb - 1)

            e.wait_ge(S["hidden_made"], 3 * NWIN * nb)
            e.dma_start(xhat[:, 0:9 * P], cw2).then_inc(S["signs2_loaded"], 16)
            e.wait_ge(S["y1_head_stored"], 16 * nb)
            e.wait_ge(S["y1_tail_stored"], 16 * nb + 16)

            def load_b(b, i):
                hold(e, S["b_lo"], b * NWIN + NWIN)
                e.dma_start(slot_(i), y1_dram[bass.ds(b + 2, 1)].rearrange("a p n -> (a p) n")
                            ).then_inc(S[f"b_loaded{i}"], 16)

            def store_b(b):
                hold(e, S["b_kept"], b * NWIN + 2 * NWIN)
                e.dma_start(y2_dram[bass.ds(b, 1)].rearrange("a p n -> (a p) n"),
                            slot_(b + 2)).then_inc(S["y2_stored"], 16)
            if streamed:
                with e.Fori(0, streamed // 2) as t:
                    for i in range(2):
                        load_b(2 * t + i, i)
                        store_b(2 * t + i)
            with e.Fori(0, (nb - streamed) // 2 - 1) as t:
                for i in range(2):
                    load_b(2 * t + streamed + i, i)

            def load_kept(k, i):
                e.dma_start(slot_(i), x3_dram[bass.ds(k + streamed, 1)].rearrange("a p n -> (a p) n")
                            ).then_inc(S[f"c_loaded{i}"], 16)

            def step_kept(k, slot, i, last):
                hold(e, S["c_relu"], k + 1)
                e.dma_start(out[bass.ds(k + streamed, 1)].rearrange("a p n -> (a p) n"), slot_(slot)
                            ).then_inc(S[f"c_stored{i}"], 16)
                if not last:
                    load_kept(k + 2, i)
            e.wait_ge(S["x3_stored"], 32 * nb + 32)
            for i in range(2):
                e.wait_ge(S["b_lo"], (nb - 1 + i) * NWIN)
                load_kept(i, i)
            kept_loop(e, step_kept)

            def load_c(t, i):
                for at, src in ((0, y2_dram), (1, x3_dram)):
                    e.dma_start(slot_(Y2_SLOTS - 2 + 2 * i + at), src[bass.ds(t * 2 + i, 1)].rearrange("a p n -> (a p) n")
                                ).then_inc(S[f"c_loaded{i}"], 16)

            def store_c(t, i):
                hold(e, S["c_relu"], t * 2 + kept_here + i + 1)
                e.dma_start(out[bass.ds(t * 2 + i, 1)].rearrange("a p n -> (a p) n"),
                            slot_(Y2_SLOTS - 2 + 2 * i)).then_inc(S[f"c_stored{i}"], 16)
            if streamed:
                e.wait_ge(S["y2_stored"], 16 * streamed)
                for i in range(2):
                    e.wait_ge(S[f"c_stored{i}"], 16 * (wrap - streamed) // 2)
                    load_c(0, i)
                if streamed > 2:
                    with e.Fori(0, streamed // 2 - 1) as t:
                        for i in range(2):
                            store_c(t, i)
                            hold(e, S[f"c_stored{i}"], 16 * t + 16 + 16 * (kept_here // 2))
                            load_c(t + 1, i)
                for i in range(2):
                    store_c(streamed // 2 - 1, i)
            for i in range(2):
                e.wait_ge(S[f"c_stored{i}"], 16 * (nb // 2))

        @block.tensor
        def _(e):
            e.wait_ge(S["vec_loaded"], 16)
            e.wait_ge(S["setup_loaded"], 128)
            e.wait_ge(S["pad_zero"], 6)
            for c in range(3):
                e.matmul(ps[:, 0, c:c + 1], wqkv_sb[:, c * P:(c + 1) * P], v_("ln1_b"), start=True, stop=True)
            for c in range(HID):
                mm = e.matmul(ps[:, 0, 3 + c:4 + c], w1_sb[:, c * P:(c + 1) * P], v_("ln2_b"), start=True, stop=True)
            mm.then_inc(S["setup_pe"], 1)

            def centre(b, n, s, src):
                if s >= 3:
                    e.wait_ge(S["squares"], (b * 2 + n) * NWIN + s - 2)
                e.matmul(ps[:, 5 + s % 3, 0:STRIP], centre_sb[:, :], src[:, s * STRIP:(s + 1) * STRIP],
                         start=True, stop=True).then_inc(S["centred"], 1)

            def variance(b, n, s):
                e.wait_ge(S["squares"], (b * 2 + n) * NWIN + s + 1)
                for i in range(LPS):
                    k = LPS * s + i
                    mm = e.matmul(ps[0:LT, 2, k:k + 1], sq[:, s % 2, i * LT:(i + 1) * LT], mean_col[:, :],
                                  start=True, stop=True)
                mm.then_inc(S["variances"], 1)

            def turn_rstd(b, n):
                hold(e, S["rstd_low"], b * 2 + n + 1)
                e.transpose(ps[0:2 * HD, 2, 2 * P:2 * P + LT], rstd_parts[:, :], eye_sb[0:LT, 0:LT]).then_inc(S["rstd_turned"], 1)

            def spread_rstd(b, n, s):
                if s == 0:
                    e.wait_ge(S["rstd_rows"], b * 2 + n + 1)
                if s >= 2:
                    e.wait_ge(S["normed"], (b * 2 + n) * NWIN + s - 1)
                for i in range(LPS):
                    k = LPS * s + i
                    mm = e.matmul(ps[:, SPREAD_BANK[n] + s % 2, i * LT:(i + 1) * LT],
                                  spread_sb[:, k:k + 1].to_broadcast([2 * HD, P]), rstd_t[:, :],
                                  start=True, stop=True)
                mm.then_inc(S["rstd_spread"], 1)

            def q_project(b, r):
                e.matmul(ps[:, 5, 0:STRIP], wqkv_sb[:, 0:P],
                         xhat[:, bass.ds(r * STRIP, STRIP)], start=True, stop=True).then_inc(S["q_made"], 1)

            def scores(b, w, half, j, queries=None):
                if queries is not None:
                    e.wait_ge(S["q_kept"], queries)
                e.wait_ge(S["k_chosen"], (b * NW + w) * TOPK + TOPK)
                slot = (half * NWIN + j) % 2
                for p in range(2):
                    mm = e.matmul(ps[:, slot, p * KEYS:(p + 1) * KEYS],
                                  q_sb[:, half, j, 2 * p:2 * p + 2, :].rearrange("p h q -> p (h q)"),
                                  ksel[:, slot, :], start=True, stop=True)
                mm.then_inc(S["scores_made"], 1)

            def lepe_place(b, t, half, k):
                if k == 0:
                    e.wait_ge(S[f"shifted{half}"], (b * SLOT_STRIPS[half] + t + 1) * ns)
                    e.wait_ge(S["lepe_kept"], b * NWIN + 2 * t + half + 1)
                ty, tx = PLACES[k]
                for g in range(HEADS):
                    src = shifted[:, half, g, :].rearrange("p (h w) -> p h w", w=VW)
                    mm = e.matmul(ps[HD * g:HD * g + HD, 6 + half, 0:STRIP], lepe_sb[:, g * NP + k, :],
                                  src[:, ty:ty + WIN, tx:tx + W], start=(k == 0), stop=(k == NP - 1))
                if k == NP - 1:
                    mm.then_inc(S["lepe_made"], 1)

            places_in = [(0,), (), (1,), (2,), (3,), (4,), ()]
            places_in_head = [(1,), (), (2,), (3,), (4,), (), ()]

            def image(b, pair, odd, first, last):
                def conv(s, taps=(0, 9)):
                    if not first:
                        binary_conv(b - 1, s, S["hi_done"], S["lo_done"], S["conv_kept"], S["conv_made"], False,
                                    3 + s % 2, taps)

                x1 = x2 = streams[odd]
                e.wait_ge(S["pos_done"], b * 9 + 9)
                centre(b, 0, 0, x1)
                for s in range(NWIN - 1):
                    centre(b, 0, s + 1, x1)
                    if s < Y1_HEAD - 1:
                        conv(s)
                    variance(b, 0, s)
                conv(Y1_HEAD - 1, (0, 3))
                variance(b, 0, NWIN - 1)
                conv(Y1_HEAD - 1, (3, 8))
                turn_rstd(b, 0)
                conv(Y1_HEAD - 1, (8, 9))

                for s in range(NWIN + 2):
                    if s < NWIN:
                        spread_rstd(b, 0, s)
                    if s < 2:
                        continue
                    k = s - 2
                    if k < 2 and not first:
                        e.wait_ge(S["conv_kept"], b * NWIN - NWIN + Y1_HEAD)
                    if k >= 2:
                        e.wait_ge(S["k_kept"], b * NWIN + k - 1)
                    e.wait_ge(S["normed"], b * 2 * NWIN + k + 1)
                    e.matmul(ps[:, 3 + k % 2, 0:STRIP], wqkv_sb[:, P:2 * P], xhat[:, k * STRIP:(k + 1) * STRIP],
                             start=True, stop=True).then_inc(S["k_made"], 1)

                q_project(b, 0)
                for s in range(NWIN):
                    if s >= 2:
                        e.wait_ge(S["v_kept"], b * NWIN + s - 1)
                    e.matmul(ps[:, 6 + s % 2, 0:STRIP], wqkv_sb[:, 2 * P:3 * P], xhat[:, s * STRIP:(s + 1) * STRIP],
                             start=True, stop=True).then_inc(S["v_made"], 1)
                    if s == 2:
                        e.wait_ge(S["k_kept"], b * NWIN + NWIN)
                    if s >= 4:
                        e.wait_ge(S["vt_kept"], (b * NWIN + s - 3) * 3)
                        e.wait_ge(S["vt_crossed"], (b * NWIN + s - 3) * 2)
                    for m in range(3):
                        e.matmul(ps[:, VT_BANKS[s % 4], m * P:(m + 1) * P],
                                 xhat[:, s * STRIP + m * P:s * STRIP + (m + 1) * P],
                                 wqkv_sb[:, 2 * P:3 * P], start=True, stop=True)
                    for o in (0, WPIX):
                        mm = e.matmul(ps[o:o + WPIX, VT_BANKS[s % 4], 3 * P:4 * P],
                                      xhat[:, s * STRIP + 6 * WPIX:s * STRIP + 7 * WPIX],
                                      wqkv_sb[:, 2 * P:3 * P], start=True, stop=True)
                    mm.then_inc(S["vt_made"], 1)
                    if s == 0:
                        e.wait_ge(S["win_sums"], b + 1)
                        e.matmul(ps[:, 2, 0:NW], wqkv_sb[:, 0:P], win_sum[:, :], start=True, stop=True)
                        e.matmul(ps[:, 2, NW:2 * NW], wqkv_sb[:, P:2 * P], win_sum[:, :], start=True,
                                 stop=True).then_inc(S["win_qk_made"], 1)
                    if s == 1:
                        e.wait_ge(S["win_qk_kept"], b * 2 + 2)
                        e.matmul(ps[0:NW, 2, 128:128 + NW], qk_win[:, 0, :], qk_win[:, 1, :], start=True,
                                 stop=True).then_inc(S["logits_made"], 1)

                e.wait_ge(S["v_kept"], b * NWIN + NWIN)
                e.wait_ge(S["vt_kept"], (b * NWIN + NWIN - 1) * 3)
                e.wait_ge(S["vt_crossed"], (b * NWIN + NWIN - 1) * 2)
                e.wait_ge(S["logits_kept"], b + 1)
                scores(b, 0, 0, 0, b * 4 * NWIN + 4)
                scores(b, 1, 0, 1)
                lepe_place(b, 0, 0, 0)

                def step(t, half, j, head, tail):
                    r = 2 * t + half
                    n = b * NW + r * NWIN + j
                    slot = (half * NWIN + j) % 2
                    e.wait_ge(S["probs_scaled"], n * 2 + 2)
                    for p in range(2):
                        for f in range(2):
                            mm = e.transpose(ps[:, 2, (2 * p + f) * P:(2 * p + f + 1) * P],
                                             probs[:, slot, p, f * P:(f + 1) * P], eye_sb[:, :])
                    mm.then_inc(S["probs_turned"], 1)
                    if j == 1 and not tail:
                        e.wait_ge(S["q_kept"], b * 4 * NWIN + r * 4 + 4)
                        q_project(b, r + 1)
                    if j < NWIN - 2:
                        scores(b, r * NWIN + j + 2, half, j + 2)
                    elif not tail:
                        scores(b, r * NWIN + j + 2, 1 - half, j + 2 - NWIN,
                               b * 4 * NWIN + r * 4 + 8 if j == NWIN - 2 else None)
                    for k in (places_in_head if head else places_in)[j]:
                        lepe_place(b, t, half, k)
                    e.wait_ge(S["turned_kept"], n + 1)
                    e.wait_ge(S["v_chosen"], n * 4 + 4)
                    if j == 0:
                        e.wait_ge(S["mixed_kept"], b * NWIN + r + 1)
                    for f in range(2):
                        for h in range(HEADS):
                            mm = e.matmul(ps[HD * h:HD * h + HD, 3 + half, j * WPIX:(j + 1) * WPIX],
                                          vsel[:, slot, f, HD * h:HD * h + HD],
                                          probs_t[:, (2 * (h // 2) + f) * P + (h % 2) * WPIX:
                                                  (2 * (h // 2) + f) * P + (h % 2 + 1) * WPIX],
                                          start=(f == 0), stop=(f == 1))
                    mm.then_inc(S["mixed"], 1)
                window_rows(e, step)

                def project(s):
                    e.wait_ge(S["lepe_tapped"], (b * NWIN + s) * 5 + 5)
                    if s >= 2:
                        e.wait_ge(S["x2_done"], b * NWIN + s - 1)
                    e.matmul(ps[:, s % 2, 0:STRIP], wo_sb[:, :], xc[:, s * STRIP:(s + 1) * STRIP], start=True,
                             stop=True).then_inc(S["projected"], 1)

                def centre2(s):
                    e.wait_ge(S["x2_done"], b * NWIN + s + 1)
                    if s == 0:
                        e.wait_ge(S["lepe_kept"], b * NWIN + NWIN + 2)
                    centre(b, 1, s, x2)
                project(0)
                project(1)
                for s in range(NWIN):
                    centre2(s)
                    if s + 2 < NWIN:
                        project(s + 2)
                    if s:
                        variance(b, 1, s - 1)
                conv(5, (0, 3))
                variance(b, 1, NWIN - 1)
                conv(5, (3, 8))
                turn_rstd(b, 1)
                conv(5, (8, 9))

                def hidden(s):
                    e.wait_ge(S["xhat_low_done"], b * NWIN + s + 1)
                    for c in range(HID):
                        if s:
                            e.wait_ge(S["hidden_kept"], b * 3 * NWIN + 3 * (s - 1) + c + 1)
                        products = [(w1_high, xhat_high(s)), (w1_high, xhat_low(s)), (w1_low, xhat_high(s))]
                        for k, (w, part) in enumerate(products):
                            mm = e.matmul(ps[:, 5 + c, 0:STRIP], w[:, c * P:(c + 1) * P], part,
                                          start=(k == 0), stop=(k == 2))
                        mm.then_inc(S["hidden_made"], 1)
                spread_rstd(b, 1, 0)
                spread_rstd(b, 1, 1)
                conv(6, (0, 5))
                spread_rstd(b, 1, 2)
                spread_rstd(b, 1, 3)
                conv(6, (5, 9))
                spread_rstd(b, 1, 4)
                spread_rstd(b, 1, 5)
                hidden(0)
                spread_rstd(b, 1, 6)
                for s in range(NWIN):
                    if s + 1 < NWIN:
                        hidden(s + 1)
                    e.wait_ge(S["hidden_kept"], b * 3 * NWIN + 3 * s + 3)
                    if s == 0:
                        e.wait_ge(S["normed"], (b * 2 + 2) * NWIN)
                    if s >= 2:
                        e.wait_ge(S["x3_done"], b * NWIN + s - 1)
                    for c in range(HID):
                        mm = e.matmul(ps[:, s % 2, 0:STRIP], w2_sb[:, c, :], hid[:, s % 2, c, :],
                                      start=(c == 0), stop=(c == HID - 1))
                    mm.then_inc(S["mlp_made"], 1)

            def binary_conv(b, s, hi_done, lo_done, kept, made, credits, bank, taps=(0, 9)):
                if taps[0] == 0:
                    have = min(s + 2, NWIN)
                    e.wait_ge(hi_done, b * NWIN + have)
                    e.wait_ge(lo_done, b * NWIN + have)
                    if credits:
                        e.wait_ge(kept, b * NWIN + s + 1)
                    elif s >= 2:
                        e.wait_ge(kept, b * NWIN + s - 1)
                for t in range(*taps):
                    dy, dx = TAPS3[t]
                    for part in (hi, lo):
                        src = part[:, :].rearrange("p (h w) -> p h w", w=CW)
                        mm = e.matmul(ps[:, bank, 0:STRIP], cw_sign[:, t, :],
                                      src[:, WIN * s + 1 + dy:WIN * s + 1 + dy + WIN, 1 + dx:1 + dx + W],
                                      start=(t == 0 and part is hi), stop=(t == 8 and part is lo))
                if taps[1] == 9:
                    mm.then_inc(made, 1)

            image_loop(e, image)
            for s in range(NWIN):
                binary_conv(nb - 1, s, S["hi_done"], S["lo_done"], S["conv_kept"], S["conv_made"], False, 3 + s % 2)

            e.sem_inc(S["b_made"], NWIN)
            e.wait_ge(S["setup_dve"], 16)
            with e.Fori(0, nb) as b:
                for s in range(NWIN):
                    binary_conv(b, s, S["b_hi"], S["b_lo"], S["b_kept"], S["b_made"], True, s)

        @block.scalar
        def _(e):
            e.sem_inc(S["b_kept"], NWIN)
            e.sem_inc(S["lepe_kept"], 2)

            def keep_centred(b, n, s):
                e.wait_ge(S["centred"], (b * 2 + n) * NWIN + s + 1)
                e.activation(xc[:, s * STRIP:(s + 1) * STRIP], ps[:, 5 + s % 3, 0:STRIP], ACT.Copy
                             ).then_inc(S["centred_copied"], 1)
                if s >= 2:
                    e.wait_ge(S["variances"], (b * 2 + n) * NWIN + s - 1)
                e.activation(sq[:, s % 2, :], ps[:, 5 + s % 3, 0:STRIP], ACT.Square).then_inc(S["squares"], 1)

            def root(b, n):
                e.wait_ge(S["eps_added"], b * 2 + n + 1)
                e.activation(ln_small[:, 1, :], ln_small[:, 0, :], ACT.Sqrt).then_inc(S["roots"], 1)

            def keep_conv(b, s):
                e.wait_ge(S["conv_made"], b * NWIN + s + 1)
                e.activation(y1(s), ps[:, 3 + s % 2, 0:STRIP],
                             ACT.Copy).then_inc(S["conv_kept"], 1)

            def q_keep(half, h):
                e.activation(q_sb[HD * h:HD * h + HD, half, :, h, :],
                             ps[HD * h:HD * h + HD, 5, 0:STRIP].rearrange("p (j q) -> p j q", q=WPIX),
                             ACT.Identity, bias=bq[HD * h:HD * h + HD, :], scale=SCALE).then_inc(S["q_kept"], 1)

            def exp(n, slot):
                e.wait_ge(S["max_found"], n + 1)
                for p in range(2):
                    e.activation(probs[:, slot, p, :], ps[:, slot, p * KEYS:(p + 1) * KEYS], ACT.Exp,
                                 bias=neg_max[:, slot, p:p + 1],
                                 accum_out=row_sum[:, slot, p:p + 1]).then_inc(S["exp_done"], 1)

            def image(b, pair, odd, first, last):
                def conv(s):
                    if not first:
                        keep_conv(b - 1, s)

                keep_centred(b, 0, 0)
                for s in range(NWIN - 1):
                    keep_centred(b, 0, s + 1)
                    if s < Y1_HEAD - 1:
                        conv(s)
                root(b, 0)
                conv(Y1_HEAD - 1)
                if not first:
                    e.wait_ge(S["y1_tail_stored"], b * 16)
                for s in range(NWIN):
                    e.wait_ge(S["k_made"], b * NWIN + s + 1)
                    e.activation(k_sb[:, s * STRIP:(s + 1) * STRIP], ps[:, 3 + s % 2, 0:STRIP], ACT.Identity,
                                 bias=bk).then_inc(S["k_kept"], 1)
                e.wait_ge(S["q_made"], b * NWIN + 1)
                for h in range(HEADS):
                    q_keep(0, h)
                for s in range(NWIN):
                    e.wait_ge(S["v_made"], b * NWIN + s + 1)
                    dst = vpad[:, :].rearrange("p (h w) -> p h w", w=VW)[:, 2 + WIN * s:2 + WIN * (s + 1), 2:2 + W]
                    e.activation(dst.rearrange("p r (x c) -> p r x c", c=WIN),
                                 ps[:, 6 + s % 2, 0:STRIP].rearrange("p (x r c) -> p r x c", r=WIN, c=WIN),
                                 ACT.Identity, bias=bv).then_inc(S["v_kept"], 1)
                    if s == 0 and not first:
                        e.wait_ge(S["y1_head_stored"], b * 16)
                    e.wait_ge(S["vt_made"], b * NWIN + s + 1)
                    made = ps[:, VT_BANKS[s % 4], 0:3 * P].rearrange("p (m c) -> p m c", c=P)
                    e.activation(vt_windows(s)[0:WPIX, 1:6:2, :], made[WPIX:P], ACT.Copy).then_inc(S["vt_crossed"], 1)
                    e.wait_ge(S["vt_kept"], (b * NWIN + s) * 3 + 1)
                    e.activation(vt_windows(s)[WPIX:P, 0:6:2, :], made[0:WPIX], ACT.Copy).then_inc(S["vt_crossed"], 1)
                exp(b * NW, 0)
                exp(b * NW + 1, 1)

                def keep_lepe(r, half):
                    e.wait_ge(S["lepe_made"], b * NWIN + r + 1)
                    e.activation(xc[:, bass.ds(r * STRIP, STRIP)], ps[:, 6 + half, 0:STRIP], ACT.Identity,
                                 bias=b_lepe).then_inc(S["lepe_kept"], 1)

                def step(t, half, j, head, tail):
                    r = 2 * t + half
                    n = b * NW + r * NWIN + j
                    slot = (half * NWIN + j) % 2
                    e.wait_ge(S["probs_turned"], n + 1)
                    e.activation(probs_t[:, :], ps[:, 2, :], ACT.Copy).then_inc(S["turned_kept"], 1)
                    if 1 <= j <= HEADS and not tail:
                        e.wait_ge(S["q_made"], b * NWIN + r + 2)
                        q_keep(1 - half, j - 1)
                    if j == NWIN - 1:
                        keep_lepe(r, half)
                    if j < NWIN - 2 or not tail:
                        exp(n + 2, slot)
                window_rows(e, step)

                for s in range(NWIN):
                    keep_centred(b, 1, s)
                root(b, 1)
                conv(5)

                def high(s):
                    e.wait_ge(S["normed"], (b * 2 + 1) * NWIN + s + 1)
                    e.activation(xhat_high(s), rows(xhat, s), ACT.Copy
                                 ).then_inc(S["xhat_high_done"], 1)
                for s in range(3):
                    high(s)
                conv(6)
                for s in range(NWIN + 1):
                    if s < NWIN:
                        if s + 3 < NWIN:
                            high(s + 3)
                        if s >= 2:
                            e.wait_ge(S["mlp_made"], b * NWIN + s - 1)
                        for c in range(HID):
                            e.wait_ge(S["hidden_made"], b * 3 * NWIN + 3 * s + c + 1)
                            e.activation(hid[:, s % 2, c, :], ps[:, 5 + c, 0:STRIP], ACT.Gelu,
                                         bias=bh[c]).then_inc(S["hidden_kept"], 1)
                    if s >= 1:
                        e.wait_ge(S["x3_done"], b * NWIN + s)
                        e.activation(inner(hi, s - 1), rows(streams[odd], s - 1), ACT.Copy).then_inc(S["hi_done"], 1)

            image_loop(e, image)
            for s in range(NWIN):
                if s == Y1_HEAD:
                    e.wait_ge(S["y1_tail_stored"], nb * 16)
                keep_conv(nb - 1, s)

            def bn_root(k):
                e.wait_ge(S["bn_dve"], k * 10 + 2)
                e.activation(bn_sb[:, 2:3], bn_sb[:, 1:2], ACT.Sqrt).then_inc(S["bn_act"], 1)

            bn_root(0)
            e.wait_ge(S["bn_dve"], 6)

            def keep_b(b, slot, s):
                e.wait_ge(S["b_made"], b * NWIN + NWIN + s + 1)
                e.activation(slot_(slot, s * STRIP, STRIP), ps[:, s, 0:STRIP], ACT.Copy).then_inc(S["b_kept"], 1)

            def image_b(b, pair, i, slot, slot_before, again):
                e.wait_ge(S[f"b_loaded{i}"], pair * 16 + 16)
                for s in range(NWIN):
                    e.wait_ge(S["b_made"], b * NWIN + min(s + 2, NWIN))
                    ys = arena[:, i * PIX + s * STRIP:i * PIX + (s + 1) * STRIP]
                    e.activation(ys, ys, ACT.Relu, bias=bn_sb[:, 5:6], scale=bn_sb[:, 4:5]).then_inc(S["relu_done"], 1)
                    e.wait_ge(S["relu_done"], b * NWIN + s + 1)
                    e.activation(inner(hi, s), ys.rearrange("p (r w) -> p r w", w=W), ACT.Copy).then_inc(S["b_hi"], 1)
                    if s == B_LAG and again is not None:
                        e.wait_ge(S["y2_stored"], again * 16 + 16)
                        e.wait_ge(S["b_stats"], again * NWIN + NWIN)
                    if s >= B_LAG:
                        keep_b(b, slot, s - B_LAG)
                    elif slot_before is not None:
                        keep_b(b - 1, slot_before, s + NWIN - B_LAG)
            image_loop_b(e, image_b)
            for s in range(NWIN - B_LAG, NWIN):
                keep_b(nb - 1, (streamed if streamed else wrap) + 1, s)
            bn_root(1)
            e.wait_ge(S["bn_dve"], 16)
            def relu_c(k, slot):
                e.wait_ge(S["c_sum"], k + 1)
                u = slot_(slot)
                e.activation(u, u, ACT.Relu, bias=bn_sb[:, 5:6]).then_inc(S["c_relu"], 1)
            kept_loop(e, lambda k, slot, i, last: relu_c(k, slot))
            if streamed:
                with e.Fori(0, streamed // 2) as t:
                    for i in range(2):
                        relu_c(2 * t + kept_here + i, Y2_SLOTS - 2 + 2 * i)

        @block.gpsimd
        def _(e):
            e.memset(q_sb[:, :, :, :, :], 0.0).then_inc(S["pad_zero"], 1)
            e.memset(vpad[:, :], 0.0).then_inc(S["pad_zero"], 1)
            e.memset(hi[:, :].bitcast(F32), 0.0).then_inc(S["pad_zero"], 1)
            e.memset(lo[:, :].bitcast(F32), 0.0).then_inc(S["pad_zero"], 1)
            e.memset(mean_col[:, :], 1.0 / P).then_inc(S["pad_zero"], 1)
            e.memset(rstd_parts[:, :], 0.0).then_inc(S["pad_zero"], 1)
            regs = [e.alloc_register(f"pool_key{i}") for i in range(TOPK)]

            def choose(b, r, slot, j):
                w = r * NWIN + j
                n = b * NW + w
                e.load(regs, key_off[0:1, bass.ds(w * TOPK, TOPK)])
                at = [e.snap(q, min_val=0, max_val=(NW - 1) * WPIX) for q in regs]
                hold(e, S["mixed"], n + 1)
                for i in range(TOPK):
                    o = WPIX * (i % 2)
                    e.tensor_copy(vsel[o:o + WPIX, slot, i // 2, :],
                                  vt[o:o + WPIX, bass.ds(at[i] * 2, P)]).then_inc(S["v_chosen"], 1)

            def image(b, pair, odd, first, last):
                hold(e, S["offsets"], b + 1)
                e.dma_start(key_off[0:1, :], top_off[:, :]).then_inc(S["offsets_placed"], 16)
                e.wait_ge(S["offsets_placed"], b * 16 + 16)
                hold(e, S["vt_kept"], b * 3 * NWIN + 3 * NWIN)
                hold(e, S["vt_crossed"], b * 2 * NWIN + 2 * NWIN)
                window_rows(e, lambda t, half, j, head, tail: choose(b, 2 * t + half, (half * NWIN + j) % 2, j))
            e.sem_inc(S["mixed"], 2)
            image_loop(e, image)

        @block.vector
        def _(e):
            order = [4, 0, 1, 2, 3, 5, 6, 7, 8]

            def pos_tap(base, k, x1):
                t = order[k]
                dy, dx = TAPS3[t]
                if k == 0:
                    e.tensor_scalar(x1, xin, pos_centre, v_("pos_b"), ALU.mult, ALU.add).then_inc(S["pos_done"], 1)
                    return
                a, i = (z.rearrange("p (h w) -> p h w", w=W) for z in (x1, xin))
                y0, y1 = max(0, -dy), H - max(0, dy)
                c0, c1 = max(0, -dx), W - max(0, dx)
                e.wait_ge(S["pos_done"], base + k)
                acc = a[:, y0:y1, c0:c1]
                e.scalar_tensor_tensor(out=acc, in0=i[:, y0 + dy:y1 + dy, c0 + dx:c1 + dx], scalar=v_("pos_w", t),
                                       in1=acc, op0=ALU.mult, op1=ALU.add).then_inc(S["pos_done"], 1)

            n_setup = [0]

            def mark(ins):
                n_setup[0] += 1
                ins.then_inc(S["setup_dve"], 1)

            e.wait_ge(S["vec_loaded"], 16)
            mark(e.tensor_scalar(pos_centre, v_("pos_w", 4), 1.0, None, ALU.add))
            e.wait_ge(S["setup_dve"], n_setup[0])
            e.wait_ge(S["x_loaded"], 16)
            for k in range(9):
                pos_tap(0, k, streams[0])

            e.wait_ge(S["setup_loaded"], 128)
            e.wait_ge(S["setup_pe"], 1)
            e.wait_ge(S["pad_zero"], 6)
            mark(e.tensor_tensor(bias[:, 0:3], ps[:, 0, 0:3], vec_sb[:, VEC["qkv_b"]:VEC["qkv_b"] + 3], ALU.add))
            mark(e.tensor_tensor(bias[:, 3:6], ps[:, 0, 3:6], vec_sb[:, VEC["mlp_b1"]:VEC["mlp_b1"] + 3], ALU.add))
            mark(e.tensor_scalar(wqkv_sb[:, :], wqkv_sb[:, :], v_("ln1_g"), None, ALU.mult))
            mark(e.tensor_scalar(w1_sb[:, :], w1_sb[:, :], v_("ln2_g"), None, ALU.mult))
            e.wait_ge(S["setup_dve"], n_setup[0])
            mark(e.tensor_copy(w1_high[:, :], w1_sb[:, :]))
            e.wait_ge(S["setup_dve"], n_setup[0])
            mark(e.tensor_tensor(w1_low[:, :], w1_sb[:, :], w1_high[:, :].bitcast(F32), ALU.subtract))
            for o in (0, HD):
                mark(e.tensor_copy(spread_sb[o:o + HD, :], eye_sb[o:o + HD, o:o + NLT]))
            mark(e.tensor_tensor(lepe_sb[:, :, :], eye4_sb[:, :].unsqueeze(1).to_broadcast([P, HEADS * NP, HD]),
                                 vec_sb[:, VEC["lepe_taps"]:VEC["lepe_taps"] + HEADS * NP].unsqueeze(2)
                                 .to_broadcast([P, HEADS * NP, HD]), ALU.mult))
            def signs():
                negative, raw = k_sb[:, 0:9 * P], xhat[:, 0:9 * P]
                mark(e.tensor_scalar(negative, raw, 0.0, None, ALU.is_lt))
                e.wait_ge(S["setup_dve"], n_setup[0])
                mark(e.scalar_tensor_tensor(out=cw_sign[:, :, :].rearrange("p t c -> p (t c)"), in0=raw,
                                            scalar=0.0, in1=negative, op0=ALU.is_gt, op1=ALU.subtract))
            signs()
            e.wait_ge(S["setup_dve"], n_setup[0])
            mark(e.tensor_tensor(b_lepe, v_("lepe_b"), bv, ALU.add))
            mark(e.tensor_scalar(bq, bq, SCALE, None, ALU.mult))
            e.wait_ge(S["setup_dve"], n_setup[0])
            e.sem_inc(S["mixed_kept"], 2)

            def rstd(b, n):
                k = b * 2 + n + 1
                e.wait_ge(S["variances"], k * NWIN)
                e.tensor_scalar(ln_small[:, 0, :], ps[0:LT, 2, 0:NLT], LN_EPS, None, ALU.add).then_inc(S["eps_added"], 1)
                e.wait_ge(S["roots"], k)
                e.reciprocal(ln_small[:, 0, :], ln_small[:, 1, :]).then_inc(S["rstd"], 1)
                e.wait_ge(S["rstd"], k)
                e.tensor_copy(rstd_parts[:, 0:NLT].bitcast(F32R), ln_small[:, 0, :]).then_inc(S["rstd_high"], 1)
                e.wait_ge(S["rstd_high"], k)
                e.tensor_tensor(rstd_parts[:, HD:HD + NLT].bitcast(F32R), ln_small[:, 0, :], rstd_parts[:, 0:NLT],
                                ALU.subtract).then_inc(S["rstd_low"], 1)
                e.wait_ge(S["rstd_turned"], k)
                e.tensor_copy(rstd_t[:, :], ps[0:2 * HD, 2, 2 * P:2 * P + LT]).then_inc(S["rstd_rows"], 1)

            def normalise(b, n, put, then=lambda s: None):
                e.wait_ge(S["centred_copied"], (b * 2 + n + 1) * NWIN)
                for s in range(NWIN):
                    e.wait_ge(S["rstd_spread"], (b * 2 + n) * NWIN + s + 1)
                    e.tensor_tensor(put(xhat, s), img(xc, s),
                                    ps[:, SPREAD_BANK[n] + s % 2, 0:STRIP].rearrange("p (r x c) -> p r x c", r=WIN, c=WIN),
                                    ALU.mult).then_inc(S["normed"], 1)
                    then(s)

            regs = [e.alloc_register(f"dve_key{i}") for i in range(TOPK)]

            def load_keys(w):
                e.load(regs, key_off[0:1, bass.ds(w * TOPK, TOPK)])

            def choose(slot):
                at = [e.snap(q, min_val=0, max_val=(NW - 1) * WPIX) for q in regs]
                for i in range(TOPK):
                    e.tensor_copy(ksel[:, slot, i * WPIX:(i + 1) * WPIX],
                                  k_sb[:, bass.ds(at[i], WPIX)]).then_inc(S["k_chosen"], 1)

            def row_max(n, slot):
                e.wait_ge(S["scores_made"], n + 1)
                e.tensor_reduce(neg_max[:, slot, :], ps[:, slot, :].rearrange("p (a k) -> p a k", a=2), AX.X,
                                ALU.max, negate=True).then_inc(S["max_found"], 1)

            def invert_sums(n, slot):
                e.wait_ge(S["exp_done"], n * 2 + 2)
                e.reciprocal(row_inv[:, slot, :], row_sum[:, slot, :]).then_inc(S["inv_done"], 1)

            def scale_probs(n, slot):
                e.wait_ge(S["inv_done"], n + 1)
                for p in range(2):
                    e.tensor_scalar(probs[:, slot, p, :], probs[:, slot, p, :], row_inv[:, slot, p:p + 1], None,
                                    ALU.mult).then_inc(S["probs_scaled"], 1)

            def conv_stats(b, s):
                e.wait_ge(S["conv_kept"], b * NWIN + s + 1)
                e.bn_stats(stats[:, bass.ds(b * NWIN + s, 1), :].rearrange("p a k -> p (a k)"),
                           y1(s)).then_inc(S["conv_stats"], 1)

            def image(b, pair, odd, first, last):
                x1 = x2 = streams[odd]

                def next_pos(*taps):
                    for k in taps:
                        if last:
                            continue
                        if k == 0:
                            e.wait_ge(S["x_loaded"], b * 16 + 32)
                            e.wait_ge(S["x3_stored"], b * 32 + 32)
                            if not first:
                                e.wait_ge(S["lo_done"], b * NWIN)
                        pos_tap(b * 9 + 9, k, streams[1 - odd])

                if not first:
                    for s in range(Y1_HEAD - 1):
                        conv_stats(b - 1, s)
                        next_pos(s)
                rstd(b, 0)
                normalise(b, 0, win)
                e.wait_ge(S["normed"], b * 2 * NWIN + NWIN)
                e.tensor_reduce(win_sum[:, :], xhat.rearrange("p (w q) -> p w q", q=WPIX), AX.X,
                                ALU.add).then_inc(S["win_sums"], 1)
                if not first:
                    conv_stats(b - 1, Y1_HEAD - 1)
                e.wait_ge(S["win_qk_made"], b + 1)
                e.tensor_scalar(qk_win[:, 0, :], ps[:, 2, 0:NW], SCALE / WPIX, bq, ALU.mult,
                                ALU.add).then_inc(S["win_qk_kept"], 1)
                e.tensor_scalar(qk_win[:, 1, :], ps[:, 2, NW:2 * NW], 1.0 / WPIX, bk, ALU.mult,
                                ALU.add).then_inc(S["win_qk_kept"], 1)
                if not first:
                    e.wait_ge(S["y1_head_stored"], b * 16)
                for s in range(NWIN):
                    e.wait_ge(S["vt_made"], b * NWIN + s + 1)
                    made = ps[:, VT_BANKS[s % 4], :].rearrange("p (m c) -> p m c", c=P)
                    e.tensor_copy(vt_windows(s)[0:WPIX, 0:7:2, :], made[0:WPIX]).then_inc(S["vt_kept"], 1)
                    e.wait_ge(S["vt_crossed"], (b * NWIN + s) * 2 + 1)
                    e.tensor_copy(vt_windows(s)[WPIX:P, 1:6:2, :], made[WPIX:P, 0:3, :]).then_inc(S["vt_kept"], 1)
                    e.tensor_copy(vt_windows(s)[WPIX:P, 6, :], made[WPIX:P, 3, :]).then_inc(S["vt_kept"], 1)
                    if s == 1:
                        e.wait_ge(S["logits_made"], b + 1)
                        e.tensor_copy(logits[:, :], ps[0:NW, 2, 128:128 + NW]).then_inc(S["logits_kept"], 1)
                        hold(e, S["logits_kept"], b + 1)
                        e.max(top8[:, :], logits[:, :]).then_inc(S["top_values"], 1)
                    if s == 2:
                        hold(e, S["top_values"], b + 1)
                        e.max_index(top_i[:, :], top8[:, :], logits[:, :]).then_inc(S["top_found"], 1)
                        e.wait_ge(S["top_found"], b + 1)
                        e.tensor_scalar(top_off[:, :], top_i[:, 0:TOPK], float(WPIX), None, ALU.mult
                                        ).then_inc(S["offsets"], 1)
                    if s == 5:
                        e.wait_ge(S["k_kept"], b * NWIN + NWIN)
                        hold(e, S["offsets_placed"], b * 16 + 16)
                        for w in range(2):
                            load_keys(w)
                            choose(w)
                    if first and s >= 3:
                        next_pos(s - 3)

                def add_mixed(r, half):
                    e.wait_ge(S["mixed"], b * NW + r * NWIN + NWIN + 2)
                    e.wait_ge(S["lepe_tapped"], (b * NWIN + r) * 5 + 2)
                    dst = xc[:, bass.ds(r * STRIP, STRIP)].rearrange("p (r x c) -> p r x c", r=WIN, c=WIN)
                    e.tensor_tensor(dst, dst, ps[:, 3 + half, 0:STRIP].rearrange("p (x r c) -> p r x c", r=WIN,
                                                                               c=WIN),
                                    ALU.add).then_inc(S["mixed_kept"], 1)

                def lepe_tap(r, k):
                    if k == 0:
                        e.wait_ge(S["lepe_kept"], b * NWIN + r + 3)
                    elif k == 2:
                        e.wait_ge(S["mixed_kept"], b * NWIN + r + 3)
                    else:
                        e.wait_ge(S["lepe_tapped"], (b * NWIN + r) * 5 + k)
                    ty, tx = RIGHT_TAPS[k]
                    src = vpad[:, bass.ds(r * WIN * VW + ty * VW, WIN * VW)].rearrange("p (h w) -> p h w", w=VW)
                    acc = xc[:, bass.ds(r * STRIP, STRIP)].rearrange("p (h w) -> p h w", w=W)
                    e.scalar_tensor_tensor(out=acc, in0=src[:, :, tx:tx + W], scalar=v_("lepe_right", k), in1=acc,
                                           op0=ALU.mult, op1=ALU.add).then_inc(S["lepe_tapped"], 1)

                def step(t, half, j, head, tail):
                    r = 2 * t + half
                    w = r * NWIN + j
                    n = b * NW + w
                    slot = (half * NWIN + j) % 2
                    ahead = j < NWIN - 2 or not tail
                    if ahead:
                        load_keys(w + 2)
                    row_max(n, slot)
                    if ahead:
                        choose(slot)
                    if not head:
                        if j in (1, 2):
                            lepe_tap(r - 1, j - 1)
                        if j == 3:
                            add_mixed(r - 1, 1 - half)
                        if j > 3:
                            lepe_tap(r - 1, j - 2)
                    invert_sums(n, slot)
                    scale_probs(n, slot)
                window_rows(e, step)

                for s in range(NWIN):
                    if s == 0:
                        lepe_tap(NWIN - 1, 0)
                        lepe_tap(NWIN - 1, 1)
                    elif s == 1:
                        add_mixed(NWIN - 1, 0)
                        lepe_tap(NWIN - 1, 2)
                    elif s < 4:
                        lepe_tap(NWIN - 1, s + 1)
                    e.wait_ge(S["projected"], b * NWIN + s + 1)
                    e.scalar_tensor_tensor(out=x2[:, s * STRIP:(s + 1) * STRIP], in0=ps[:, s % 2, 0:STRIP],
                                           scalar=v_("wo_b"), in1=x1[:, s * STRIP:(s + 1) * STRIP], op0=ALU.add,
                                           op1=ALU.add).then_inc(S["x2_done"], 1)
                next_pos(4)
                rstd(b, 1)

                def low(s):
                    e.wait_ge(S["xhat_high_done"], b * NWIN + s + 1)
                    e.tensor_tensor(xhat_low(s), rows(xhat, s),
                                    xhat_high(s).bitcast(F32), ALU.subtract).then_inc(S["xhat_low_done"], 1)
                normalise(b, 1, img, then=lambda s: low(s - 3) if s in (3, 4, 5) else None)
                if not first:
                    for s in range(Y1_HEAD, NWIN):
                        conv_stats(b - 1, s)
                for s in range(NWIN):
                    if s + 3 < NWIN:
                        low(s + 3)
                    e.wait_ge(S["mlp_made"], b * NWIN + s + 1)
                    xs = x2[:, s * STRIP:(s + 1) * STRIP]
                    e.scalar_tensor_tensor(out=xs, in0=ps[:, s % 2, 0:STRIP], scalar=v_("mlp_b2"), in1=xs,
                                           op0=ALU.add, op1=ALU.add).then_inc(S["x3_done"], 1)
                    if s in (0, 1, 3, 4):
                        next_pos((0, 1, 3, 4).index(s) + 5)
                    e.wait_ge(S["hi_done"], b * NWIN + s + 1)
                    e.tensor_tensor(inner(lo, s), rows(x2, s), inner(hi, s).bitcast(F32),
                                    ALU.subtract).then_inc(S["lo_done"], 1)

            image_loop(e, image)
            for s in range(NWIN):
                conv_stats(nb - 1, s)

            def batch_norm(k, counted, gamma, beta):
                def m(ins, n):
                    ins.then_inc(S["bn_dve"], n)
                e.wait_ge(counted, nb * NWIN)
                m(e.bn_aggr(bn_sb[:, 0:2], stats[:, :, :].rearrange("p a k -> p (a k)")), 1)
                e.wait_ge(S["bn_dve"], k * 10 + 1)
                m(e.tensor_scalar(bn_sb[:, 1:2], bn_sb[:, 1:2], BN_EPS, None, ALU.add), 1)
                e.wait_ge(S["bn_act"], k + 1)
                m(e.reciprocal(bn_sb[:, 3:4], bn_sb[:, 2:3]), 1)
                e.wait_ge(S["bn_dve"], k * 10 + 3)
                if k:
                    e.wait_ge(S["relu_done"], nb * NWIN)
                m(e.tensor_tensor(bn_sb[:, 4:5], bn_sb[:, 3:4], gamma, ALU.mult), 1)
                e.wait_ge(S["bn_dve"], k * 10 + 4)
                m(e.tensor_tensor(bn_sb[:, 2:3], bn_sb[:, 0:1], bn_sb[:, 4:5], ALU.mult), 1)
                e.wait_ge(S["bn_dve"], k * 10 + 5)
                m(e.tensor_tensor(bn_sb[:, 5:6], beta, bn_sb[:, 2:3], ALU.subtract), 5)

            batch_norm(0, S["conv_stats"], v_("gamma1"), v_("beta1"))
            e.wait_ge(S["signs2_loaded"], 16)
            signs()

            def stats_b(b, slot, s):
                e.wait_ge(S["b_kept"], b * NWIN + NWIN + s + 1)
                e.bn_stats(stats[:, bass.ds(b * NWIN + s, 1), :].rearrange("p a k -> p (a k)"),
                           slot_(slot, s * STRIP, STRIP)).then_inc(S["b_stats"], 1)

            def image_b(b, pair, i, slot, slot_before, again):
                for s in range(NWIN):
                    e.wait_ge(S["b_hi"], b * NWIN + s + 1)
                    e.tensor_tensor(inner(lo, s), rows(arena[:, i * PIX:(i + 1) * PIX], s),
                                    inner(hi, s).bitcast(F32), ALU.subtract).then_inc(S["b_lo"], 1)
                    if s > B_LAG:
                        stats_b(b, slot, s - B_LAG - 1)
                    elif slot_before is not None:
                        stats_b(b - 1, slot_before, s + NWIN - B_LAG - 1)
            image_loop_b(e, image_b)
            for s in range(NWIN - B_LAG - 1, NWIN):
                stats_b(nb - 1, (streamed if streamed else wrap) + 1, s)
            batch_norm(1, S["b_stats"], v_("gamma2"), v_("beta2"))
            e.wait_ge(S["bn_dve"], 20)

            def sum_c(y2, x3):
                e.scalar_tensor_tensor(out=y2, in0=y2, scalar=bn_sb[:, 4:5], in1=x3, op0=ALU.mult,
                                       op1=ALU.add).then_inc(S["c_sum"], 1)

            def sum_kept(k, slot, i, last):
                e.wait_ge(S[f"c_loaded{i}"], (k - i) * 8 + 16)
                sum_c(slot_(slot), slot_(i))
            kept_loop(e, sum_kept)
            if streamed:
                with e.Fori(0, streamed // 2) as t:
                    for i in range(2):
                        e.wait_ge(S[f"c_loaded{i}"], 32 * t + 32 + 8 * kept_here)
                        sum_c(slot_(Y2_SLOTS - 2 + 2 * i), slot_(Y2_SLOTS - 1 + 2 * i))


def lay_out(inputs, nb):
    f = {k: np.asarray(v) for k, v in inputs.items()}
    vec = np.zeros((P, NVEC), np.float32)

    def put(name, a, k=1):
        vec[:, VEC[name]:VEC[name] + k] = a

    L0 = "L0_conv_"
    put("pos_w", f[L0 + "pos_w"].reshape(P, 9), 9)
    for name in ("pos_b", "ln1_g", "ln1_b", "lepe_b", "wo_b", "ln2_g", "ln2_b", "mlp_b2"):
        put(name, f[L0 + name].reshape(P, 1))
    put("qkv_b", f[L0 + "qkv_b"].reshape(3, P).T, 3)
    put("mlp_b1", f[L0 + "mlp_b1"].reshape(HID, P).T, HID)
    for name in ("gamma1", "beta1", "gamma2", "beta2"):
        put(name, f["L1_conv_" + name].reshape(P, 1))
    lepe = f[L0 + "lepe_w"].reshape(P, 5, 5)
    for t, (ty, tx) in enumerate(PLACES):
        for k, (sy, sx) in enumerate(SHIFTS):
            for g in range(HEADS):
                vec[HD * k:HD * k + HD, VEC["lepe_taps"] + g * NP + t] = lepe[HD * g:HD * g + HD, ty + sy, tx + sx]
    for t, (ty, tx) in enumerate(RIGHT_TAPS):
        vec[:, VEC["lepe_right"] + t] = lepe[:, ty, tx]

    def conv(w):
        return np.ascontiguousarray(w.transpose(1, 2, 3, 0).reshape(P, 9 * P))

    eye = np.eye(P, dtype=np.float32)
    return {
        "x": np.ascontiguousarray(f["x"].reshape(-1, P, PIX)[:nb]),
        "vec": vec,
        "wqkv": f[L0 + "qkv_w"], "wo": f[L0 + "wo_w"], "w1": f[L0 + "mlp_w1"], "w2": f[L0 + "mlp_w2"],
        "cw1": conv(f["L1_conv_w1"]), "cw2": conv(f["L1_conv_w2"]),
        "eye": eye, "centre": eye - np.float32(1.0 / P), "eye4": np.tile(eye[0:HD, 0:HD], (4, 1)),
    }


def kernel(**inputs):
    import concourse.bacc as _bacc
    from concourse.bass_utils import run_bass_kernel_spmd as _run

    nb = inputs["x"].shape[0]
    arrays = lay_out(inputs, nb)
    nc = _bacc.Bacc("TRN2", target_bir_lowering=False, num_devices=1)
    aps = {n: nc.dram_tensor(n, a.shape, F32, kind="ExternalInput").ap() for n, a in arrays.items()}
    out = nc.dram_tensor("out", (nb, P, PIX), F32, kind="ExternalOutput").ap()
    build(nc, **aps, out=out, nb=nb)
    r = _run(nc, [arrays], core_ids=[0])
    return r.results[0]["out"].reshape(nb, P, H, W)
```
